# Optimizing a Trainium2 kernel written in Bass

```python
import numpy as np
import jax
import jax.numpy as jnp

def _softmax(x, axis=-1):
    return jax.nn.softmax(x, axis=axis)

def _gelu(x):
    return jax.nn.gelu(x, approximate=True)

def _silu(x):
    return jax.nn.silu(x)

def _sigmoid(x):
    return jax.nn.sigmoid(x)

def _layernorm(x, axis=-1, eps=1e-05):
    m = jnp.mean(x, axis=axis, keepdims=True)
    v = jnp.var(x, axis=axis, keepdims=True)
    return (x - m) / jnp.sqrt(v + eps)

def _scatter_add(tgt, idx, src, axis=0):
    return tgt.at[idx].add(src)

def _segment_sum(src, seg, n):
    return jax.ops.segment_sum(src, seg, n)
kernel_name = 'mk_gnn_ffn_d2_gnn_r32_a381c6'

def setup_inputs(seed: int=0):
    np.random.seed(seed)
    _w = jnp.asarray

    def _rec_inputs():
        import jax
        import jax.numpy as jnp
        _gk = jax.random.key(seed)
        x = -0.0002117 + 1 * jax.random.normal(jax.random.fold_in(_gk, 1), (3125, 256), jnp.float32)
        src = jax.random.randint(jax.random.fold_in(_gk, 2), (50000,), 0, 3125, jnp.int32)
        dst = jax.random.randint(jax.random.fold_in(_gk, 3), (50000,), 0, 3125, jnp.int32)
        _o = jnp.argsort(dst, stable=True)
        src = src[_o]
        dst = dst[_o]
        edge_attr_16 = -9.77346e-05 + 0.999888 * jax.random.normal(jax.random.fold_in(_gk, 13), (50000, 16), jnp.float32)
        return (x, src, dst, edge_attr_16)
    x, src, dst, edge_attr_16 = _rec_inputs()

    def _L0_gnn_setup():
        import jax, jax.numpy as jnp
        import numpy as np
        N_NODES = 3125
        N_EDGES = 100000
        NODE_F = 256
        EDGE_F = 16
        N_HEAD = 8
        OUT_F = 256
        NEG_SLOPE = 0.2
        BN_EPS = 1e-05

        def _seg_softmax(e, idx, num_segments):
            m = jax.ops.segment_max(e, idx, num_segments=num_segments)
            ex = jnp.exp(e - m[idx])
            s = jax.ops.segment_sum(ex, idx, num_segments=num_segments)
            return ex / s[idx]
        key = jax.random.key(seed)
        ks = jax.random.split(key, 16)
        inp = {}
        inp['feat_src'] = jax.random.normal(ks[0], (N_NODES, NODE_F), jnp.float32)
        inp['feat_edge'] = jax.random.normal(ks[1], (N_EDGES, EDGE_F), jnp.float32)
        inp['src'] = jax.random.randint(ks[2], (N_EDGES,), 0, N_NODES, jnp.int32)
        inp['dst'] = jax.random.randint(ks[3], (N_EDGES,), 0, N_NODES, jnp.int32)

        def xav(k, fan_in, fan_out):
            std = np.sqrt(2.0) * np.sqrt(2.0 / (fan_in + fan_out))
            return jax.random.normal(k, (fan_in, fan_out), jnp.float32) * std
        inp['W_prop_src'] = xav(ks[4], NODE_F, N_HEAD)
        inp['W_attn_src'] = xav(ks[5], NODE_F, N_HEAD)
        inp['W_attn_dst'] = xav(ks[6], NODE_F, N_HEAD)
        inp['W_attn_edge'] = xav(ks[7], EDGE_F, N_HEAD)
        inp['bn_gamma'] = jnp.ones((N_HEAD,), jnp.float32)
        inp['bn_beta'] = jnp.zeros((N_HEAD,), jnp.float32)
        inp['W_agg'] = xav(ks[8], N_HEAD, OUT_F)
        inp['b_agg'] = jnp.zeros((OUT_F,), jnp.float32)
        inp['W_apply_dst'] = xav(ks[9], NODE_F, OUT_F)
        inp['b_apply_dst'] = jnp.zeros((OUT_F,), jnp.float32)
        inp['W_apply'] = xav(ks[10], OUT_F, OUT_F)
        inp['b_apply'] = jnp.zeros((OUT_F,), jnp.float32)
        return inp
    _L0_gnn_all = _L0_gnn_setup()
    _L0_gnn_in = {k: v for k, v in _L0_gnn_all.items() if k in ('W_prop_src', 'W_attn_src', 'W_attn_dst', 'W_attn_edge', 'bn_gamma', 'bn_beta', 'W_agg', 'b_agg', 'W_apply_dst', 'b_apply_dst', 'W_apply', 'b_apply')}
    del _L0_gnn_all

    def _L0_ffn_setup():
        import jax, jax.numpy as jnp
        import numpy as np
        D_MODEL = 256
        EXPERT_DIM = 512
        NUM_EXPERTS = 8
        TOP_K = 2
        SEQ_LEN = 64
        BATCH = 2
        key = jax.random.key(seed)
        ks = jax.random.split(key, 8)
        s = 0.02
        x = jax.random.normal(ks[0], (SEQ_LEN, BATCH, D_MODEL), dtype=jnp.float32)
        Wg = jax.random.normal(ks[1], (D_MODEL, NUM_EXPERTS), dtype=jnp.float32) * s
        bg = jax.random.normal(ks[2], (NUM_EXPERTS,), dtype=jnp.float32) * s
        bias = jnp.zeros((NUM_EXPERTS,), dtype=jnp.float32)
        W1 = jax.random.normal(ks[3], (NUM_EXPERTS, D_MODEL, EXPERT_DIM), dtype=jnp.float32) * s
        b1 = jax.random.normal(ks[4], (NUM_EXPERTS, EXPERT_DIM), dtype=jnp.float32) * s
        W2 = jax.random.normal(ks[5], (NUM_EXPERTS, EXPERT_DIM, D_MODEL), dtype=jnp.float32) * s
        b2 = jax.random.normal(ks[6], (NUM_EXPERTS, D_MODEL), dtype=jnp.float32) * s
        return {'x': x, 'Wg': Wg, 'bg': bg, 'bias': bias, 'W1': W1, 'b1': b1, 'W2': W2, 'b2': b2}
    _L0_ffn_all = _L0_ffn_setup()
    _L0_ffn_in = {k: v for k, v in _L0_ffn_all.items() if k in ('Wg', 'bg', 'bias', 'W1', 'b1', 'W2', 'b2')}
    del _L0_ffn_all

    def _L1_gnn_setup():
        import jax, jax.numpy as jnp
        import numpy as np
        N, E = (50000, 25000)
        IN_C, HID_C, OUT_C = (256, 256, 256)

        def _gcn_prep(edge_index, n_nodes):
            src = jnp.concatenate([edge_index[0], jnp.arange(n_nodes, dtype=edge_index.dtype)])
            dst = jnp.concatenate([edge_index[1], jnp.arange(n_nodes, dtype=edge_index.dtype)])
            deg = jax.ops.segment_sum(jnp.ones_like(dst, dtype=jnp.float32), dst, num_segments=n_nodes)
            deg_inv_sqrt = jnp.where(deg > 0, jax.lax.rsqrt(jnp.maximum(deg, 1.0)), 0.0)
            norm = deg_inv_sqrt[src] * deg_inv_sqrt[dst]
            return (src, dst, norm)

        def _gcn_layer(x, src, dst, norm, W, b, n_nodes):
            h = x @ W
            msg = h[src] * norm[:, None]
            out = jax.ops.segment_sum(msg, dst, num_segments=n_nodes)
            return out + b
        key = jax.random.key(seed)
        ks = jax.random.split(key, 8)
        x_piece = jax.random.normal(ks[0], (N, IN_C), dtype=jnp.float32)
        edge_index_piece = jax.random.randint(ks[1], (2, E), 0, N, dtype=jnp.int64)
        batch = jnp.zeros((N,), dtype=jnp.int64)

        def glorot(k, fan_in, fan_out):
            s = jnp.sqrt(6.0 / (fan_in + fan_out)).astype(jnp.float32)
            return jax.random.uniform(k, (fan_in, fan_out), jnp.float32, -s, s)
        return {'x_piece': x_piece, 'edge_index_piece': edge_index_piece, 'batch': batch, 'W1': glorot(ks[2], IN_C, HID_C), 'b1': jnp.zeros((HID_C,), jnp.float32), 'W2': glorot(ks[3], HID_C, HID_C), 'b2': jnp.zeros((HID_C,), jnp.float32), 'W3': glorot(ks[4], HID_C, OUT_C), 'b3': jnp.zeros((OUT_C,), jnp.float32)}
    _L1_gnn_all = _L1_gnn_setup()
    _L1_gnn_in = {k: v for k, v in _L1_gnn_all.items() if k in ('W1', 'b1', 'W2', 'b2', 'W3', 'b3')}
    del _L1_gnn_all

    def _L1_ffn_setup():
        import math
        import jax, jax.numpy as jnp
        import numpy as np
        CAPACITY_FACTOR = 1.25
        key = jax.random.key(seed)
        ks = jax.random.split(key, 5)
        B, L, D, F, E = (8, 256, 256, 1024, 8)
        h = jax.random.normal(ks[0], (B, L, D), dtype=jnp.float32)
        gate_w = jax.random.normal(ks[1], (D, E), dtype=jnp.float32) * 0.02
        gate_b = jnp.zeros((E,), dtype=jnp.float32)
        w1 = jax.random.normal(ks[2], (E, D, F), dtype=jnp.float32) * (1.0 / math.sqrt(D))
        b1 = jnp.zeros((E, F), dtype=jnp.float32)
        w2 = jax.random.normal(ks[3], (E, F, D), dtype=jnp.float32) * (1.0 / math.sqrt(F))
        b2 = jnp.zeros((E, D), dtype=jnp.float32)
        return {'h': h, 'gate_w': gate_w, 'gate_b': gate_b, 'w1': w1, 'b1': b1, 'w2': w2, 'b2': b2}
    _L1_ffn_all = _L1_ffn_setup()
    _L1_ffn_in = {k: v for k, v in _L1_ffn_all.items() if k in ('gate_w', 'gate_b', 'w1', 'b1', 'w2', 'b2')}
    del _L1_ffn_all
    return {'x': x, 'src': src, 'dst': dst, 'edge_attr_16': edge_attr_16, 'L0_gnn_W_prop_src': _L0_gnn_in['W_prop_src'], 'L0_gnn_W_attn_src': _L0_gnn_in['W_attn_src'], 'L0_gnn_W_attn_dst': _L0_gnn_in['W_attn_dst'], 'L0_gnn_W_attn_edge': _L0_gnn_in['W_attn_edge'], 'L0_gnn_bn_gamma': _L0_gnn_in['bn_gamma'], 'L0_gnn_bn_beta': _L0_gnn_in['bn_beta'], 'L0_gnn_W_agg': _L0_gnn_in['W_agg'], 'L0_gnn_b_agg': _L0_gnn_in['b_agg'], 'L0_gnn_W_apply_dst': _L0_gnn_in['W_apply_dst'], 'L0_gnn_b_apply_dst': _L0_gnn_in['b_apply_dst'], 'L0_gnn_W_apply': _L0_gnn_in['W_apply'], 'L0_gnn_b_apply': _L0_gnn_in['b_apply'], 'L0_ffn_Wg': _L0_ffn_in['Wg'], 'L0_ffn_bg': _L0_ffn_in['bg'], 'L0_ffn_bias': _L0_ffn_in['bias'], 'L0_ffn_W1': _L0_ffn_in['W1'], 'L0_ffn_b1': _L0_ffn_in['b1'], 'L0_ffn_W2': _L0_ffn_in['W2'], 'L0_ffn_b2': _L0_ffn_in['b2'], 'L1_gnn_W1': _L1_gnn_in['W1'], 'L1_gnn_b1': _L1_gnn_in['b1'], 'L1_gnn_W2': _L1_gnn_in['W2'], 'L1_gnn_b2': _L1_gnn_in['b2'], 'L1_gnn_W3': _L1_gnn_in['W3'], 'L1_gnn_b3': _L1_gnn_in['b3'], 'L1_ffn_gate_w': _L1_ffn_in['gate_w'], 'L1_ffn_gate_b': _L1_ffn_in['gate_b'], 'L1_ffn_w1': _L1_ffn_in['w1'], 'L1_ffn_b1': _L1_ffn_in['b1'], 'L1_ffn_w2': _L1_ffn_in['w2'], 'L1_ffn_b2': _L1_ffn_in['b2']}

def reference(x, src, dst, edge_attr_16, L0_gnn_W_prop_src, L0_gnn_W_attn_src, L0_gnn_W_attn_dst, L0_gnn_W_attn_edge, L0_gnn_bn_gamma, L0_gnn_bn_beta, L0_gnn_W_agg, L0_gnn_b_agg, L0_gnn_W_apply_dst, L0_gnn_b_apply_dst, L0_gnn_W_apply, L0_gnn_b_apply, L0_ffn_Wg, L0_ffn_bg, L0_ffn_bias, L0_ffn_W1, L0_ffn_b1, L0_ffn_W2, L0_ffn_b2, L1_gnn_W1, L1_gnn_b1, L1_gnn_W2, L1_gnn_b2, L1_gnn_W3, L1_gnn_b3, L1_ffn_gate_w, L1_ffn_gate_b, L1_ffn_w1, L1_ffn_b1, L1_ffn_w2, L1_ffn_b2):
    import jax
    import jax.numpy as jnp

    def _L0_gnn_ref(feat_src, feat_edge, src, dst, W_prop_src, W_attn_src, W_attn_dst, W_attn_edge, bn_gamma, bn_beta, W_agg, b_agg, W_apply_dst, b_apply_dst, W_apply, b_apply):
        import jax, jax.numpy as jnp
        import numpy as np
        N_NODES = 3125
        N_EDGES = 100000
        NODE_F = 256
        EDGE_F = 16
        N_HEAD = 8
        OUT_F = 256
        NEG_SLOPE = 0.2
        BN_EPS = 1e-05

        def _seg_softmax(e, idx, num_segments):
            m = jax.ops.segment_max(e, idx, num_segments=num_segments)
            ex = jnp.exp(e - m[idx])
            s = jax.ops.segment_sum(ex, idx, num_segments=num_segments)
            return ex / s[idx]
        leaky = lambda x: jnp.where(x >= 0, x, NEG_SLOPE * x)
        feat_dst = feat_src
        feat_src_fc = feat_src @ W_prop_src
        attn_src = feat_src @ W_attn_src
        attn_dst = feat_dst @ W_attn_dst
        attn_edge = feat_edge @ W_attn_edge
        e = attn_src[src] + attn_dst[dst] + attn_edge
        e = leaky(e)
        a_dst = jnp.clip(_seg_softmax(e, dst, N_NODES), 1e-09)
        a_src = jnp.clip(_seg_softmax(e, src, N_NODES), 1e-09)
        a = jnp.sqrt(a_dst * a_src)
        msg_sum = jax.ops.segment_sum(feat_src_fc[src] * a, dst, num_segments=N_NODES)
        mu = jnp.mean(msg_sum, axis=0)
        var = jnp.mean((msg_sum - mu) ** 2, axis=0)
        h = (msg_sum - mu) / jnp.sqrt(var + BN_EPS) * bn_gamma + bn_beta
        rst = h @ W_agg + b_agg
        rst = rst + feat_dst @ W_apply_dst + b_apply_dst
        rst = leaky(rst)
        rst = rst @ W_apply + b_apply
        return rst

    def _L0_ffn_ref(x, Wg, bg, bias, W1, b1, W2, b2):
        import jax, jax.numpy as jnp
        import numpy as np
        D_MODEL = 256
        EXPERT_DIM = 512
        NUM_EXPERTS = 8
        TOP_K = 2
        SEQ_LEN = 64
        BATCH = 2
        x_flat = x.reshape(-1, D_MODEL)
        gate_logits = x_flat @ Wg + bg + bias
        topk_vals, topk_idx = jax.lax.top_k(gate_logits, TOP_K)
        topk_w = jax.nn.softmax(topk_vals, axis=-1)
        combine = (jax.nn.one_hot(topk_idx, NUM_EXPERTS, dtype=x.dtype) * topk_w[..., None]).sum(axis=1)
        h = jax.nn.relu(jnp.einsum('td,edh->teh', x_flat, W1) + b1)
        y = jnp.einsum('teh,ehd->ted', h, W2) + b2
        out = jnp.einsum('ted,te->td', y, combine)
        return out.reshape(x.shape)

    def _L1_gnn_ref(x_piece, edge_index_piece, batch, W1, b1, W2, b2, W3, b3):
        import jax, jax.numpy as jnp
        import numpy as np
        N, E = (50000, 25000)
        IN_C, HID_C, OUT_C = (256, 256, 256)

        def _gcn_prep(edge_index, n_nodes):
            src = jnp.concatenate([edge_index[0], jnp.arange(n_nodes, dtype=edge_index.dtype)])
            dst = jnp.concatenate([edge_index[1], jnp.arange(n_nodes, dtype=edge_index.dtype)])
            deg = jax.ops.segment_sum(jnp.ones_like(dst, dtype=jnp.float32), dst, num_segments=n_nodes)
            deg_inv_sqrt = jnp.where(deg > 0, jax.lax.rsqrt(jnp.maximum(deg, 1.0)), 0.0)
            norm = deg_inv_sqrt[src] * deg_inv_sqrt[dst]
            return (src, dst, norm)

        def _gcn_layer(x, src, dst, norm, W, b, n_nodes):
            h = x @ W
            msg = h[src] * norm[:, None]
            out = jax.ops.segment_sum(msg, dst, num_segments=n_nodes)
            return out + b
        n_nodes = x_piece.shape[0]
        src, dst, norm = _gcn_prep(edge_index_piece, n_nodes)
        x = _gcn_layer(x_piece, src, dst, norm, W1, b1, n_nodes)
        x = jax.nn.gelu(x)
        x = _gcn_layer(x, src, dst, norm, W2, b2, n_nodes)
        x = jax.nn.gelu(x)
        x = _gcn_layer(x, src, dst, norm, W3, b3, n_nodes)
        return x

    def _L1_ffn_ref(h, gate_w, gate_b, w1, b1, w2, b2):
        import math
        import jax, jax.numpy as jnp
        import numpy as np
        CAPACITY_FACTOR = 1.25
        B, L, D = h.shape
        E = gate_w.shape[1]
        T = B * L
        C = max(1, math.ceil(CAPACITY_FACTOR * T / E))
        x = h.reshape(T, D)
        logits = x @ gate_w + gate_b
        probs = jax.nn.softmax(logits, axis=-1)
        idx = jnp.argmax(probs, axis=-1)
        prb = jnp.take_along_axis(probs, idx[:, None], axis=1)[:, 0]
        one_hot = jax.nn.one_hot(idx, E, dtype=jnp.float32)
        pos = (jnp.cumsum(one_hot, axis=0) * one_hot).sum(-1).astype(jnp.int32) - 1
        kept = pos < C
        pos_safe = jnp.where(kept, pos, C)
        buf = jnp.zeros((E, C, D), dtype=h.dtype).at[idx, pos_safe].set(x, mode='drop')
        hmid = jax.nn.relu(jnp.einsum('ecd,edf->ecf', buf, w1) + b1[:, None, :])
        ybuf = jnp.einsum('ecf,efd->ecd', hmid, w2) + b2[:, None, :]
        pos_g = jnp.minimum(pos, C - 1)
        y_tok = ybuf[idx, pos_g] * (prb * kept)[:, None]
        y = y_tok.reshape(B, L, D)
        y = jnp.nan_to_num(y, nan=0.0, posinf=10000.0, neginf=-10000.0)
        return y
    edge_index = jnp.stack([src, dst])
    batch0 = jnp.zeros((3125,), jnp.int32)
    x = x + _L0_gnn_ref(_layernorm(x, axis=-1), edge_attr_16, src, dst, L0_gnn_W_prop_src, L0_gnn_W_attn_src, L0_gnn_W_attn_dst, L0_gnn_W_attn_edge, L0_gnn_bn_gamma, L0_gnn_bn_beta, L0_gnn_W_agg, L0_gnn_b_agg, L0_gnn_W_apply_dst, L0_gnn_b_apply_dst, L0_gnn_W_apply, L0_gnn_b_apply)
    x = x + _L0_ffn_ref(_layernorm(x, axis=-1)[None], L0_ffn_Wg, L0_ffn_bg, L0_ffn_bias, L0_ffn_W1, L0_ffn_b1, L0_ffn_W2, L0_ffn_b2)[0]
    x = x + _L1_gnn_ref(_layernorm(x, axis=-1), edge_index, batch0, L1_gnn_W1, L1_gnn_b1, L1_gnn_W2, L1_gnn_b2, L1_gnn_W3, L1_gnn_b3)
    x = x + _L1_ffn_ref(_layernorm(x, axis=-1)[None], L1_ffn_gate_w, L1_ffn_gate_b, L1_ffn_w1, L1_ffn_b1, L1_ffn_w2, L1_ffn_b2)[0]
    return x

_drawn_inputs = setup_inputs


def setup_inputs(seed=0):
    import zlib

    import numpy as np

    out = dict(_drawn_inputs(seed))
    spreads = {'L0_gnn_bn_gamma': (1.0, 0.2),
     'L0_gnn_bn_beta': (0.0, 0.286),
     'L0_gnn_b_agg': (0.0, 0.1),
     'L0_gnn_b_apply_dst': (0.0, 0.1),
     'L0_gnn_b_apply': (0.0, 0.1),
     'L0_ffn_bias': (0.0, 0.277),
     'L1_gnn_b1': (0.0, 0.35),
     'L1_gnn_b2': (0.0, 0.1),
     'L1_gnn_b3': (0.0, 0.1),
     'L1_ffn_gate_b': (0.0, 0.1),
     'L1_ffn_b1': (0.0, 0.8),
     'L1_ffn_b2': (0.0, 0.8)}
    factors = {'L0_ffn_bg': 18.233, 'L0_ffn_b1': 8.0, 'L0_ffn_b2': 5.666}
    for name, (base, spread) in spreads.items():
        noise = np.random.default_rng([zlib.crc32(name.encode()), seed]).standard_normal(out[name].shape)
        drawn = base * np.exp(spread * noise) if base else spread * noise
        out[name] = jnp.asarray(drawn.astype(out[name].dtype))
    for name, factor in factors.items():
        out[name] = (out[name] * factor).astype(out[name].dtype)
    return out
```

```python
from contextlib import ExitStack

import concourse.bass as bass
from concourse import mybir

F32 = mybir.dt.float32
I32 = mybir.dt.int32
U32 = mybir.dt.uint32
BF16 = mybir.dt.bfloat16
F16 = mybir.dt.float16
ALU = mybir.AluOpType
ACT = mybir.ActivationFunctionType
AX = mybir.AxisListType

N, D, E, H, FE = 3125, 256, 50000, 8, 16
P = 125
NJ = N // P
EC = E // P
KD = D // 128
G = 20
NB = EC // G
LN_EPS, BN_EPS = 1e-5, 1e-5
SLOPE, CLIP = 0.2, 1e-9
BIG = 1e38
ROUND = 12582912.0
SKIP = float(1 << 20)
NEXP = 8
X0F = 512


def build(nc, a, out):
    top = ExitStack()
    used = []
    ps = [top.enter_context(nc.psum_tensor(f"bank{i}", [128, 512], F32)) for i in range(8)]

    def dram(name, shape, dt=F32):
        return nc.dram_tensor(name, shape, dt, kind="Internal").ap()

    def sb_in(ctx, tag=""):
        return lambda name, shape, dt=F32: ctx.enter_context(nc.sbuf_tensor(tag + name, shape, dt))

    def sem_in(ctx, tag=""):
        def sem(name):
            used.append(nc.alloc_semaphore(tag + name))
            return used[-1]
        return sem

    def recycle():
        nc.all_engine_barrier()
        nc.clear_and_free_semaphores(list(used))
        used.clear()
        nc.all_engine_barrier()

    def chain(eng, sem):
        at = [0]

        def link(ins):
            at[0] += 1
            ins.then_inc(sem, 1)
            eng.wait_ge(sem, at[0])
        return link

    keep = sb_in(top)
    x = keep("x", [P, NJ, D])
    ident = keep("ident", [128, 128])
    before = keep("before", [P, P])
    lower = keep("lower", [P, P])
    ones = keep("ones", [P, EC])
    dinv = keep("dinv", [P, NJ])
    window = keep("window", [P, NJ + 1])
    key_cols = dram("key_cols", (2, E))
    xnT = keep("xnT", [128, KD, NJ, P])

    def constants():
        with ExitStack() as ctx:
            sem = sem_in(ctx, "k_")
            zero_set, made, x_in = sem("zero_set"), sem("made"), sem("x_in")
            block = ctx.enter_context(nc.Block())

            @block.sync
            def _(sp):
                sp.dma_start(x[:, :, :], a["x"].rearrange("(p j) d -> p j d", j=NJ)).then_inc(x_in, 16)
                sp.wait_ge(x_in, 16)

            @block.gpsimd
            def _(pool):
                pool.memset(ident[:, :], 0.0).then_inc(zero_set, 1)
                pool.memset(before[:, :], 1.0).then_inc(zero_set, 1)
                pool.memset(ones[:, :], 1.0)
                pool.memset(lower[:, :], 1.0).then_inc(zero_set, 1)
                pool.wait_ge(zero_set, 3)
                pool.affine_select(out=ident[:, :], in_=ident[:, :], compare_op=ALU.not_equal, fill=1.0,
                                   base=0, pattern=[[-1, 128]], channel_multiplier=1).then_inc(made, 1)
                pool.affine_select(out=before[:, :], in_=before[:, :], compare_op=ALU.is_gt, fill=0.0,
                                   base=0, pattern=[[1, P]], channel_multiplier=-1).then_inc(made, 1)
                pool.affine_select(out=lower[:, :], in_=lower[:, :], compare_op=ALU.is_gt, fill=0.0,
                                   base=0, pattern=[[-1, P]], channel_multiplier=1).then_inc(made, 1)
                pool.wait_ge(made, 3)

    def norm_transpose(tag, xn):
        with ExitStack() as ctx:
            sb, sem = sb_in(ctx, tag), sem_in(ctx, tag)
            stats = sb("stats", [P, NJ, 6])
            mv = sb("mv", [P, NJ, 2])
            rstd = sb("rstd", [P, NJ])
            own, var_ready, dev_ready = sem("own"), sem("var_ready"), sem("dev_ready")
            xn_ready, turned, kept = sem("xn_ready"), sem("turned"), sem("kept")
            block = ctx.enter_context(nc.Block())

            @block.vector
            def _(dve):
                link = chain(dve, own)
                for j in range(NJ - 1):
                    nc.vector.bn_stats(stats[:, j, :], x[:, j, :])
                link(nc.vector.bn_stats(stats[:, NJ - 1, :], x[:, NJ - 1, :]))
                for j in range(NJ - 1):
                    nc.vector.bn_aggr(mv[:, j, :], stats[:, j, :])
                link(nc.vector.bn_aggr(mv[:, NJ - 1, :], stats[:, NJ - 1, :]))
                nc.vector.tensor_scalar(rstd[:, :], mv[:, :, 1], LN_EPS, None, ALU.add).then_inc(var_ready, 1)
                dve.wait_ge(dev_ready, 1)
                link(nc.vector.reciprocal(rstd[:, :], rstd[:, :]))
                for j in range(NJ):
                    nc.vector.tensor_scalar(xn[:, j, :], x[:, j, :], mv[:, j, 0:1], rstd[:, j:j + 1],
                                            ALU.subtract, ALU.mult).then_inc(xn_ready, 1)

            @block.tensor
            def _(pe):
                for j in range(NJ):
                    pe.wait_ge(xn_ready, j + 1)
                    if j >= 8:
                        pe.wait_ge(kept, j - 7)
                    for k in range(KD):
                        t = nc.tensor.transpose(ps[j % 8][:, k * P:(k + 1) * P],
                                                xn[:, j, k * 128:(k + 1) * 128], ident[0:P, 0:P])
                    t.then_inc(turned, 1)

            @block.scalar
            def _(act):
                act.wait_ge(var_ready, 1)
                nc.scalar.activation(rstd[:, :], rstd[:, :], ACT.Sqrt).then_inc(dev_ready, 1)
                for j in range(NJ):
                    act.wait_ge(turned, j + 1)
                    nc.scalar.activation(xnT[:, :, j, :], ps[j % 8][:, 0:KD * P].rearrange("q (k p) -> q k p", k=KD),
                                         ACT.Copy).then_inc(kept, 1)

    def layer0_gnn():
        with ExitStack() as layer:
            sbl = sb_in(layer)
            nodes = sbl("nodes", [P, NJ, 3 * H])
            base_s, deg_s = sbl("base_s", [P, NJ]), sbl("deg_s", [P, NJ])
            base_d, deg_d = sbl("base_d", [P, NJ]), sbl("deg_d", [P, NJ])
            pos = sbl("pos", [P, EC])
            keys = sbl("keys", [P, 2, EC])
            by_src = dram("by_src", (E, H + 2))
            starts_s = dram("starts_s", (E, 2 * H))
            starts_d = dram("starts_d", (E, H))
            from_src = dram("from_src", (E, 3 * H))
            sums_d = dram("sums_d", (E, H))

            project_nodes(nodes)
            rank_edges(keys, pos, base_s, deg_s, base_d, deg_d)
            with ExitStack() as dctx:
                fd = flag_tiles(dctx, "fd_")
                flags("fd_", a["dst"].unsqueeze(1), 0, I32, fd)
                edge_terms(nodes, base_s, deg_s, base_d, deg_d, keys, pos, fd, by_src, starts_s, starts_d)
            with ExitStack() as sctx:
                fs = flag_tiles(sctx, "fs_")
                vs = sb_in(sctx)("vs", [P, EC, H + 2])
                flags("fs_", by_src, H, F32, fs, vs)
                rows = sb_in(sctx)("rows_s", [P, EC, 3 * H])
                source_softmax(fs, rows, vs, starts_s, from_src)
                degrees(deg_d)
            recycle()
            with ExitStack() as dctx:
                fd = flag_tiles(dctx, "fe_")
                flags("fe_", a["dst"].unsqueeze(1), 0, I32, fd)
                got = sb_in(dctx)("rows_d", [P, EC, 3 * H])
                gather_rows(got, pos, from_src)
                msg = sb_in(dctx)("msg", [P, NJ, H])
                target_softmax(fd, got, sums_d, base_d, deg_d, msg)
                apply_nodes(msg)

    def project_nodes(nodes):
        with ExitStack() as ctx:
            sb, sem = sb_in(ctx, "pn_"), sem_in(ctx, "pn_")
            w = sb("w", [128, KD, 3 * H])
            w_in, done, kept = sem("w_in"), sem("done"), sem("kept")
            block = ctx.enter_context(nc.Block())

            @block.sync
            def _(sp):
                for n, name in enumerate(("L0_gnn_W_prop_src", "L0_gnn_W_attn_src", "L0_gnn_W_attn_dst")):
                    sp.dma_start(w[:, :, n * H:(n + 1) * H], a[name].rearrange("(k q) h -> q k h", k=KD)).then_inc(w_in, 16)

            @block.tensor
            def _(pe):
                pe.wait_ge(w_in, 48)
                for j in range(NJ):
                    bank, at = ps[j // 20], (j % 20) * 3 * H
                    for k in range(KD):
                        m = nc.tensor.matmul(bank[0:P, at:at + 3 * H], xnT[:, k, j, :], w[:, k, :],
                                             start=k == 0, stop=k == KD - 1)
                    m.then_inc(done, 1)

            @block.vector
            def _(dve):
                for b, (lo, hi) in enumerate(((0, 20), (20, NJ))):
                    dve.wait_ge(done, hi)
                    nc.vector.tensor_copy(nodes[:, lo:hi, :], ps[b][0:P, 0:(hi - lo) * 3 * H].rearrange(
                        "p (j h) -> p j h", h=3 * H)).then_inc(kept, 1)
                dve.wait_ge(kept, 2)

    def rank_edges(keys, pos, base_s, deg_s, base_d, deg_d):
        with ExitStack() as ctx:
            sb, sem = sb_in(ctx, "rk_"), sem_in(ctx, "rk_")
            hot_js = sb("hot_js", [P, EC, NJ], BF16)
            counts = sb("counts", [P, EC + 1, NJ])
            srcf = sb("srcf", [P, EC])
            centre = sb("centre", [P, 1])
            first = ExitStack()
            sb1 = sb_in(first, "rk1_")
            hot_jd = sb1("hot_jd", [P, EC, NJ], BF16)
            ids = sb1("ids", [P, 2, EC], I32)
            lane25 = sb1("lane25", [P, 2, EC])
            tmp = sb1("tmp", [P, 2, EC])
            iota_i = sb1("iota_i", [P, P], I32)
            iota_p = sb1("iota_p", [P, P])
            iota_ji = sb1("iota_ji", [P, NJ], I32)
            iota_j = sb1("iota_j", [P, NJ])
            centre_i = sb1("centre_i", [P, 1], I32)
            zero_b = sb1("zero_b", [P, P], BF16)
            hot_s = sb1("hot_s", [P, 2, G, P], BF16)
            hot_d = sb1("hot_d", [P, 2, G, P], BF16)
            tot = sb1("tot", [P, 2, NJ])
            incl = sb1("incl", [P, 2, NJ])
            own = sem("own")
            ids_in, iotas, ready = sem("ids_in"), sem("iotas"), sem("ready")
            hot_ready = sem("hot_ready")
            counted, counts_kept, all_counted = sem("counted"), sem("counts_kept"), sem("all_counted")
            lane_tot, lane_base = sem("lane_tot"), sem("lane_base")
            with nc.Block() as block:
                @block.sync
                def _(sp):
                    sp.dma_start(ids[:, 0, :], a["src"].rearrange("(p c) -> p c", c=EC)).then_inc(ids_in, 16)
                    sp.dma_start(ids[:, 1, :], a["dst"].rearrange("(p c) -> p c", c=EC)).then_inc(ids_in, 16)

                @block.gpsimd
                def _(pool):
                    pool.memset(zero_b[:, :], 0.0)
                    pool.iota(iota_i[:, :], [[NJ, P]], base=0, channel_multiplier=0)
                    pool.iota(iota_ji[:, :], [[1, NJ]], base=0, channel_multiplier=0)
                    pool.iota(centre_i[:, :], [[1, 1]], base=-(NJ // 2), channel_multiplier=-NJ).then_inc(iotas, 1)

                @block.vector
                def _(dve):
                    link = chain(dve, own)
                    dve.wait_ge(iotas, 1)
                    nc.vector.tensor_copy(iota_p[:, :], iota_i[:, :])
                    nc.vector.tensor_copy(centre[:, :], centre_i[:, :])
                    nc.vector.tensor_copy(iota_j[:, :], iota_ji[:, :])
                    dve.wait_ge(ids_in, 32)
                    nc.vector.tensor_copy(srcf[:, :], ids[:, 0, :])
                    link(nc.vector.tensor_scalar(tmp[:, :, :], ids[:, :, :], 1.0 / NJ, -0.48, ALU.mult, ALU.add))
                    link(nc.vector.tensor_scalar(tmp[:, :, :], tmp[:, :, :], ROUND, ROUND, ALU.add, ALU.subtract))
                    nc.vector.tensor_scalar(lane25[:, :, :], tmp[:, :, :], float(NJ), None, ALU.mult)
                    link(nc.vector.tensor_scalar(keys[:, :, :], ids[:, :, :], float(P), None, ALU.mult))
                    link(nc.vector.scalar_tensor_tensor(out=keys[:, :, :], in0=tmp[:, :, :], scalar=1.0 - NJ * P, in1=keys[:, :, :],
                                                        op0=ALU.mult, op1=ALU.add))
                    link(nc.vector.tensor_tensor(tmp[:, :, :], ids[:, :, :], lane25[:, :, :], ALU.subtract))
                    for o, hot_j in enumerate((hot_js, hot_jd)):
                        last = nc.vector.tensor_tensor(hot_j[:, :, :], tmp[:, o, :].unsqueeze(2).to_broadcast([P, EC, NJ]),
                                                       iota_j[:, :].unsqueeze(1).to_broadcast([P, EC, NJ]), ALU.is_equal)
                    last.then_inc(ready, 1)
                    with dve.Fori(0, NB // 2) as b:
                        for u in range(2):
                            dve.wait_ge(counted, 2 * b + u + 1)
                            for o, hot in enumerate((hot_s, hot_d)):
                                last = nc.vector.tensor_tensor(
                                    hot[:, u, :, :], lane25[:, o, bass.ds((2 * b + u) * G, G)].unsqueeze(2).to_broadcast([P, G, P]),
                                    iota_p[:, :].unsqueeze(1).to_broadcast([P, G, P]), ALU.is_equal)
                            last.then_inc(hot_ready, 1)
                    dve.wait_ge(counts_kept, NB + 2)
                    dve.wait_ge(all_counted, 1)
                    nc.vector.tensor_reduce(tot[:, 0, :], counts[:, 1:EC + 1, :].rearrange("p c j -> p j c"), AX.X, ALU.add)
                    link(nc.vector.tensor_copy(tot[:, 1, :], ps[4][0:P, 0:NJ]))
                    link(nc.vector.tensor_tensor_scan(incl[:, 1, :], ones[:, 0:NJ], tot[:, 1, :], 0.0, ALU.mult, ALU.add))
                    nc.vector.tensor_copy(deg_s[:, :], tot[:, 0, :])
                    nc.vector.tensor_copy(deg_d[:, :], tot[:, 1, :])
                    nc.vector.tensor_tensor(tmp[:, 1, 0:NJ], incl[:, 1, :], tot[:, 1, :], ALU.subtract).then_inc(lane_tot, 1)
                    dve.wait_ge(lane_base, 1)
                    nc.vector.tensor_scalar(base_d[:, :], tmp[:, 1, 0:NJ], ps[5][0:P, 64:65], None, ALU.add)
                    nc.vector.memset(window[:, 0:1], 0.0)
                    link(nc.vector.tensor_tensor_scan(window[:, 1:NJ + 1], ones[:, 0:NJ], ps[5][0:P, 32:32 + NJ], 0.0, ALU.mult, ALU.add))
                    nc.vector.tensor_tensor(base_s[:, :], window[:, 0:NJ], ps[5][0:P, 0:NJ], ALU.add)
                    link(nc.vector.tensor_tensor(counts[:, 0, :], window[:, 0:NJ], ps[5][0:P, 0:NJ], ALU.add))
                    for j in range(NJ):
                        last = nc.vector.tensor_tensor_scan(counts[:, 1:EC + 1, j], ones[:, :], counts[:, 1:EC + 1, j],
                                                            base_s[:, j:j + 1], ALU.mult, ALU.add)
                    link(last)

                @block.scalar
                def _(act):
                    act.sem_inc(counts_kept, 2)
                    with act.Fori(0, NB // 2) as b:
                        for u in range(2):
                            act.wait_ge(counted, 2 * b + u + 3)
                            nc.scalar.activation(counts[:, bass.ds((2 * b + u) * G + 1, G), :],
                                                 ps[u][0:P, 0:G * NJ].rearrange("p (g j) -> p g j", j=NJ),
                                                 ACT.Copy).then_inc(counts_kept, 1)

                @block.tensor
                def _(pe):
                    pe.wait_ge(ready, 1)
                    pe.sem_inc(counted, 2)
                    nc.tensor.matmul(ps[4][0:P, 0:NJ], zero_b[:, :], zero_b[:, 0:NJ], start=True, stop=False)
                    with pe.Fori(0, NB // 2) as b:
                        for u in range(2):
                            pe.wait_ge(hot_ready, 2 * b + u + 1)
                            pe.wait_ge(counts_kept, 2 * b + u + 1)
                            for g in range(G):
                                c = (2 * b + u) * G + g
                                nc.tensor.matmul(ps[u][0:P, g * NJ:(g + 1) * NJ], hot_s[:, u, g, :],
                                                 hot_js[:, bass.ds(c, 1), :].rearrange("p a j -> p (a j)"),
                                                 start=True, stop=True)
                                m = nc.tensor.matmul(ps[4][0:P, 0:NJ], hot_d[:, u, g, :],
                                                     hot_jd[:, bass.ds(c, 1), :].rearrange("p a j -> p (a j)"),
                                                     start=False, stop=False)
                            m.then_inc(counted, 1)
                    nc.tensor.matmul(ps[4][0:P, 0:NJ], zero_b[:, :], zero_b[:, 0:NJ], start=False, stop=True).then_inc(all_counted, 1)
                    pe.wait_ge(lane_tot, 1)
                    nc.tensor.matmul(ps[5][0:P, 0:NJ], before[:, :], tot[:, 0, :], start=True, stop=True)
                    nc.tensor.matmul(ps[5][0:P, 32:32 + NJ], ones[:, 0:P], tot[:, 0, :], start=True, stop=True)
                    nc.tensor.matmul(ps[5][0:P, 64:65], before[:, :], incl[:, 1, NJ - 1:NJ], start=True, stop=True).then_inc(lane_base, 1)

            first.close()
            row = sb("row", [P, 2, G * P], I32)
            dist = sb("dist", [P, 2, G * P])
            hot_t = sb("hot_t", [P, 2, G, P])
            picked = sb("picked", [P, 2, G, NJ])
            same = sb("same", [P, 2, G, P], BF16)
            intra = sb("intra", [P, EC])
            row_in = [sem("row_in0"), sem("row_in1")]
            dist_ready, hot_t_ready, looked_up, row_done = sem("dist_ready"), sem("hot_t_ready"), sem("looked_up"), sem("row_done")
            picks, own2 = sem("picks"), sem("own2")
            with nc.Block() as block:
                @block.sync
                def _(sp):
                    with sp.Fori(0, NB // 2) as b:
                        for u in range(2):
                            sp.wait_ge(row_done, 2 * b + u + 1)
                            sp.dma_start(row[:, u, :], a["src_cols"][bass.ds(2 * b + u, 1), :].to_broadcast([P, G * P])).then_inc(row_in[u], 16)

                @block.scalar
                def _(act):
                    with act.Fori(0, NB // 2) as b:
                        for u in range(2):
                            act.wait_ge(row_in[u], 16 * b + 16)
                            act.wait_ge(hot_t_ready, 2 * b + u + 1)
                            nc.scalar.activation(dist[:, u, :], row[:, u, :], ACT.Square, bias=centre[:, 0:1]).then_inc(dist_ready, 1)

                @block.vector
                def _(dve):
                    dve.sem_inc(row_done, 2)
                    dve.sem_inc(picks, 2)
                    dve.sem_inc(hot_t_ready, 2)
                    with dve.Fori(0, NB // 2) as b:
                        for u in range(2):
                            at = 2 * b + u
                            dve.wait_ge(dist_ready, at + 1)
                            dve.wait_ge(looked_up, at + 1)
                            nc.vector.tensor_scalar(hot_t[:, u, :, :].rearrange("p g q -> p (g q)"), dist[:, u, :],
                                                    float((NJ // 2) ** 2) + 1.0, None, ALU.is_le).then_inc(hot_t_ready, 1)
                            for g in range(G):
                                c = at * G + g
                                last = nc.vector.scalar_tensor_tensor(
                                    out=same[:, u, g, :], in0=row[:, u, g * P:(g + 1) * P], scalar=srcf[:, bass.ds(c, 1)],
                                    in1=lower[:, :], op0=ALU.is_equal, op1=ALU.mult, accum_out=intra[:, bass.ds(c, 1)])
                            last.then_inc(row_done, 1)
                            dve.wait_ge(looked_up, at + 3)
                            nc.vector.tensor_tensor(picked[:, u, :, :], ps[u][0:P, 0:G * NJ].rearrange("p (g j) -> p g j", j=NJ),
                                                    hot_js[:, bass.ds(at * G, G), :], ALU.mult).then_inc(picks, 1)
                            dve.wait_ge(picks, at + 3)
                            nc.vector.tensor_reduce(pos[:, bass.ds(at * G, G)], picked[:, u, :, :], AX.X, ALU.add).then_inc(own2, 1)
                    dve.wait_ge(own2, NB)
                    nc.vector.tensor_tensor(pos[:, :], pos[:, :], intra[:, :], ALU.add).then_inc(own2, 1)
                    dve.wait_ge(own2, NB + 1)

                @block.tensor
                def _(pe):
                    pe.sem_inc(looked_up, 2)
                    with pe.Fori(0, NB // 2) as b:
                        for u in range(2):
                            at = 2 * b + u
                            pe.wait_ge(hot_t_ready, at + 3)
                            pe.wait_ge(picks, at + 1)
                            for g in range(G):
                                m = nc.tensor.matmul(ps[u][0:P, g * NJ:(g + 1) * NJ], hot_t[:, u, g, :],
                                                     counts[:, bass.ds(at * G + g, 1), :].rearrange("p a j -> p (a j)"),
                                                     start=True, stop=True)
                            m.then_inc(looked_up, 1)

    class Flags:
        pass

    def flag_tiles(ctx, tag):
        sb, f = sb_in(ctx, tag), Flags()
        f.go_on, f.back_on = sb("go_on", [P, EC]), sb("back_on", [P, EC])
        f.drop = sb("drop", [P, EC])
        f.ends = sb("ends", [P, EC])
        f.head, f.head_drop = sb("head", [P, EC]), sb("head_drop", [P, EC])
        f.tail = sb("tail", [P, EC])
        f.through = sb("through", [2 * H, 3, P])
        return f

    def flags(tag, table, col, dt, f, whole=None):
        with ExitStack() as ctx:
            sb, sem = sb_in(ctx, tag), sem_in(ctx, tag)
            key = sb("key", [P, EC + 2], dt)
            wide = sb("wide", [P, 3, 2 * H])
            key_set, keys_in, own, wide_ready, turned = sem("key_set"), sem("keys_in"), sem("own"), sem("wide_ready"), sem("turned")
            block = ctx.enter_context(nc.Block())
            lanes = table[:, col:col + 1].rearrange("(p c) a -> p (c a)", c=EC)

            @block.sync
            def _(sp):
                if whole is None:
                    sp.dma_start(key[:, 1:EC + 1], lanes).then_inc(keys_in, 16)
                else:
                    sp.dma_start(whole[:, :, :], table.rearrange("(p c) h -> p c h", c=EC)).then_inc(keys_in, 16)
                sp.wait_ge(key_set, 1)
                sp.dma_start(key[1:P, 0:1], lanes[0:P - 1, EC - 1:EC], allow_slow_non_contiguous=True).then_inc(keys_in, 16)
                sp.dma_start(key[0:P - 1, EC + 1:EC + 2], lanes[1:P, 0:1], allow_slow_non_contiguous=True).then_inc(keys_in, 16)

            @block.vector
            def _(dve):
                link = chain(dve, own)
                nc.vector.memset(key[:, 0:1], -1)
                nc.vector.memset(key[:, EC + 1:EC + 2], -1).then_inc(key_set, 1)
                dve.wait_ge(keys_in, 48)
                if whole is not None:
                    link(nc.vector.tensor_copy(key[:, 1:EC + 1], whole[:, :, col]))
                link(nc.vector.tensor_tensor(f.go_on[:, :], key[:, 1:EC + 1], key[:, 0:EC], ALU.is_equal))
                link(nc.vector.tensor_tensor(f.back_on[:, :], key[:, 1:EC + 1], key[:, 2:EC + 2], ALU.is_equal))
                nc.vector.tensor_scalar(f.drop[:, :], f.go_on[:, :], 1.0, BIG, ALU.subtract, ALU.mult)
                nc.vector.tensor_scalar(f.ends[:, :], f.back_on[:, :], -1.0, 1.0, ALU.mult, ALU.add)
                nc.vector.tensor_tensor_scan(f.tail[:, ::-1], f.back_on[:, ::-1], ones[:, :], 1.0, ALU.mult, ALU.mult)
                link(nc.vector.tensor_tensor_scan(f.head[:, :], f.go_on[:, :], ones[:, :], 1.0, ALU.mult, ALU.mult))
                link(nc.vector.tensor_scalar(f.head_drop[:, :], f.head[:, :], 1.0, BIG, ALU.subtract, ALU.mult))
                for n, t in enumerate((f.head[:, EC - 1:EC], f.head_drop[:, EC - 1:EC], f.tail[:, 0:1])):
                    last = nc.vector.tensor_copy(wide[:, n, :], t.to_broadcast([P, 2 * H]))
                last.then_inc(wide_ready, 1)
                dve.wait_ge(turned, 1)
                link(nc.vector.tensor_copy(f.through[:, :, :], ps[0][0:2 * H, 0:3 * P].rearrange("h (n p) -> h n p", p=P)))

            @block.tensor
            def _(pe):
                pe.wait_ge(wide_ready, 1)
                for n in range(3):
                    t = nc.tensor.transpose(ps[0][0:2 * H, n * P:(n + 1) * P], wide[:, n, :], ident[0:P, 0:P])
                t.then_inc(turned, 1)

    def scan_runs(tag, f, v, n, kind):
        with ExitStack() as ctx:
            sb, sem = sb_in(ctx, tag), sem_in(ctx, tag)
            carry = sb("carry", [2 * H, P + 1])
            own, scanned, carried, turned, back = sem("own"), sem("scanned"), sem("carried"), sem("turned"), sem("back")
            block = ctx.enter_context(nc.Block())
            forward = kind != "end"
            on, op = {"sum": (f.go_on, ALU.add), "max": (f.drop, ALU.max), "end": (f.back_on, ALU.add)}[kind]
            by, lane_on = (ALU.add, 1) if kind == "max" else (ALU.mult, 0 if forward else 2)
            reach = {"sum": f.head, "max": f.head_drop, "end": f.tail}[kind]
            start = -BIG if kind == "max" else 0.0
            edge = EC - 1 if forward else 0
            step = slice(None) if forward else slice(None, None, -1)

            @block.vector
            def _(dve):
                link = chain(dve, own)
                nc.vector.memset(carry[0:n, :], start)
                for h in range(n):
                    last = nc.vector.tensor_tensor_scan(v[:, step, h], on[:, step], v[:, step, h], start, by, op)
                last.then_inc(scanned, 1)
                dve.wait_ge(turned, 1)
                inner = carry[0:n, 1:P + 1] if forward else carry[0:n, 0:P]
                nc.vector.tensor_tensor_scan(inner[:, step], f.through[0:n, lane_on, step], ps[0][0:n, 0:P][:, step],
                                             start, by, op).then_inc(carried, 1)
                dve.wait_ge(back, 1)
                for h in range(n):
                    last = nc.vector.scalar_tensor_tensor(out=v[:, :, h], in0=reach[:, :], scalar=ps[1][0:P, h:h + 1],
                                                          in1=v[:, :, h], op0=by, op1=op)
                link(last)

            @block.tensor
            def _(pe):
                pe.wait_ge(scanned, 1)
                nc.tensor.transpose(ps[0][0:n, 0:P], v[:, edge, 0:n], ident[0:P, 0:P]).then_inc(turned, 1)
                pe.wait_ge(carried, 1)
                nc.tensor.transpose(ps[1][0:P, 0:n], carry[0:n, 0:P] if forward else carry[0:n, 1:P + 1],
                                    ident[0:n, 0:n]).then_inc(back, 1)

    def run_total(tag, f, v, kind):
        scan_runs(tag + "f_", f, v, H, kind)
        with ExitStack() as ctx:
            done = sem_in(ctx, tag)("done")
            block = ctx.enter_context(nc.Block())

            @block.vector
            def _(dve):
                nc.vector.tensor_tensor(v[:, :, :], v[:, :, :], f.ends[:, :].unsqueeze(2).to_broadcast([P, EC, H]),
                                        ALU.mult).then_inc(done, 1)
                dve.wait_ge(done, 1)
        scan_runs(tag + "b_", f, v, H, "end")

    def softmax_runs(tag, f, e, out_a, ctx):
        m = sb_in(ctx, tag)("m", [P, EC, H])
        with ExitStack() as c2:
            done = sem_in(c2, tag)("copied")
            block = c2.enter_context(nc.Block())

            @block.vector
            def _(dve):
                nc.vector.tensor_copy(m[:, :, :], e).then_inc(done, 1)
                dve.wait_ge(done, 1)
        run_total(tag + "m", f, m, "max")
        ex = sb_in(ctx, tag)("ex", [P, EC, H])
        with ExitStack() as c2:
            sem = sem_in(c2, tag)
            less, done, own = sem("less"), sem("exps"), sem("own")
            block = c2.enter_context(nc.Block())

            @block.vector
            def _(dve):
                nc.vector.tensor_tensor(ex[:, :, :], e, m[:, :, :], ALU.subtract).then_inc(less, 1)
                dve.wait_ge(done, 1)
                nc.vector.tensor_copy(m[:, :, :], ex[:, :, :]).then_inc(own, 1)
                dve.wait_ge(own, 1)

            @block.scalar
            def _(act):
                act.wait_ge(less, 1)
                nc.scalar.activation(ex[:, :, :], ex[:, :, :], ACT.Exp).then_inc(done, 1)
        run_total(tag + "s", f, m, "sum")
        with ExitStack() as c2:
            own = sem_in(c2, tag)("own3")
            block = c2.enter_context(nc.Block())

            @block.vector
            def _(dve):
                link = chain(dve, own)
                link(nc.vector.reciprocal(m[:, :, :], m[:, :, :]))
                link(nc.vector.tensor_tensor(ex[:, :, :], ex[:, :, :], m[:, :, :], ALU.mult))
                link(nc.vector.tensor_scalar(out_a, ex[:, :, :], CLIP, None, ALU.max))

    def zero_dram(tag, tables):
        with ExitStack() as ctx:
            sb, sem = sb_in(ctx, tag), sem_in(ctx, tag)
            z = sb("z", [P, EC * 2 * H])
            set_, done = sem("set"), sem("done")
            block = ctx.enter_context(nc.Block())

            @block.gpsimd
            def _(pool):
                pool.memset(z[:, :], 0.0).then_inc(set_, 1)

            @block.sync
            def _(sp):
                sp.wait_ge(set_, 1)
                for t in tables:
                    w = t.shape[1]
                    sp.dma_start(t.rearrange("(p c) h -> p (c h)", c=EC), z[:, 0:EC * w]).then_inc(done, 16)
                sp.wait_ge(done, 16 * len(tables))

    def edge_terms(nodes, base_s, deg_s, base_d, deg_d, keys, pos, fd, by_src, starts_s, starts_d):
        zero_dram("z_", (starts_s, starts_d))
        with ExitStack() as outer:
            sbo = sb_in(outer, "et_")
            v = sbo("v", [P, EC, H])
            row = sbo("row", [P, EC, H + 2])
            where = sbo("where", [P, 2, NJ], I32)
            tmpf = sbo("tmpf", [P, 2, NJ])
            with ExitStack() as ctx:
                sem = sem_in(ctx, "et_")
                own, where_ready, spread, v_in = sem("own"), sem("where_ready"), sem("spread"), sem("v_in")
                block = ctx.enter_context(nc.Block())

                @block.vector
                def _(dve):
                    link = chain(dve, own)
                    for o, (base, deg) in enumerate(((base_s, deg_s), (base_d, deg_d))):
                        link(nc.vector.tensor_scalar(tmpf[:, o, :], deg[:, :], 0.0, SKIP, ALU.is_equal, ALU.mult))
                        link(nc.vector.tensor_tensor(tmpf[:, o, :], tmpf[:, o, :], base[:, :], ALU.add))
                    nc.vector.tensor_copy(where[:, :, :], tmpf[:, :, :]).then_inc(where_ready, 1)

                @block.gpsimd
                def _(pool):
                    pool.wait_ge(where_ready, 1)
                    for o, (table, cols) in enumerate(((starts_s, slice(0, 2 * H)), (starts_d, slice(2 * H, 3 * H)))):
                        for j in range(NJ):
                            pool.indirect_dma_start(table, bass.IndirectOffsetOnAxis(ap=where[:, o, j:j + 1].bitcast(U32), axis=0),
                                                    nodes[:, j, cols], None, bounds_check=E - 1, oob_is_err=False).then_inc(spread, 16)

                @block.sync
                def _(sp):
                    sp.wait_ge(spread, 2 * NJ * 16)
                    sp.dma_start(v[:, :, :], starts_d.rearrange("(p c) h -> p c h", c=EC)).then_inc(v_in, 16)
                    sp.wait_ge(v_in, 16)
            scan_runs("etd_", fd, v, H, "sum")
            with ExitStack() as ctx:
                sb, sem = sb_in(ctx, "ea_"), sem_in(ctx, "ea_")
                attr = sb("attr", [128, EC // 8, P])
                w8 = sb("w8", [128, 8, H])
                w_set, w_in, attr_in, done = sem("w_set"), sem("w_in"), sem("attr_in"), sem("done")
                added, own = sem("added"), sem("own")
                block = ctx.enter_context(nc.Block())

                @block.sync
                def _(sp):
                    sp.dma_start(attr[:, :, :], a["edge_attr_cols"]).then_inc(attr_in, 16)
                    sp.wait_ge(w_set, 1)
                    for c in range(8):
                        sp.dma_start(w8[c * FE:(c + 1) * FE, c, :], a["L0_gnn_W_attn_edge"]).then_inc(w_in, 16)

                @block.tensor
                def _(pe):
                    pe.wait_ge(w_in, 8 * 16)
                    pe.wait_ge(attr_in, 16)
                    for b in range(EC // 8):
                        if b >= 8:
                            pe.wait_ge(added, b - 7)
                        nc.tensor.matmul(ps[b % 8][0:P, 0:8 * H], attr[:, b, :], w8[:, :, :].rearrange("q c h -> q (c h)"),
                                         start=True, stop=True).then_inc(done, 1)

                @block.vector
                def _(dve):
                    nc.vector.memset(w8[:, :, :], 0.0).then_inc(w_set, 1)
                    nc.vector.tensor_copy(row[:, :, H:H + 2], keys[:, :, :].rearrange("p o c -> p c o"))
                    for b in range(EC // 8):
                        dve.wait_ge(done, b + 1)
                        nc.vector.tensor_tensor(row[:, b * 8:(b + 1) * 8, 0:H], v[:, b * 8:(b + 1) * 8, :],
                                                ps[b % 8][0:P, 0:8 * H].rearrange("p (c h) -> p c h", h=H), ALU.add).then_inc(added, 1)
                    dve.wait_ge(added, EC // 8)
            with ExitStack() as ctx:
                sb, sem = sb_in(ctx, "sc_"), sem_in(ctx, "sc_")
                ring = sb("ring", [P, 2, G, H + 2])
                index = sb("index", [P, 2, G], I32)
                staged, sent, gate = sem("staged"), [sem("sent0"), sem("sent1")], sem("gate")
                block = ctx.enter_context(nc.Block())

                @block.vector
                def _(dve):
                    for u in range(2):
                        nc.vector.tensor_copy(ring[:, u, :, :], row[:, u * G:(u + 1) * G, :])
                        nc.vector.tensor_copy(index[:, u, :], pos[:, u * G:(u + 1) * G]).then_inc(staged, 1)
                    with dve.Fori(1, NB // 2) as b:
                        for u in range(2):
                            dve.wait_ge(sent[u], b * (16 * G))
                            nc.vector.tensor_copy(ring[:, u, :, :], row[:, bass.ds((2 * b + u) * G, G), :])
                            nc.vector.tensor_copy(index[:, u, :], pos[:, bass.ds((2 * b + u) * G, G)]).then_inc(staged, 1)

                @block.gpsimd
                def _(pool):
                    with pool.Fori(0, NB // 2) as b:
                        for u in range(2):
                            pool.wait_ge(staged, 2 * b + u + 1)
                            pool.sem_inc(gate, 1)
                            for g in range(G):
                                pool.indirect_dma_start(by_src, bass.IndirectOffsetOnAxis(ap=index[:, u, g:g + 1].bitcast(U32), axis=0),
                                                        ring[:, u, g, :], None).then_inc(sent[u], 16)
                    for u in range(2):
                        pool.wait_ge(sent[u], NB // 2 * 16 * G)

    def source_softmax(fs, rows, vs, starts_s, from_src):
        with ExitStack() as ctx:
            compact = sb_in(ctx, "kc_")("compact", [P, 2, EC])
            sem = sem_in(ctx, "kc_")
            own, sent = sem("own"), sem("sent")
            block = ctx.enter_context(nc.Block())

            @block.vector
            def _(dve):
                nc.vector.tensor_copy(compact[:, :, :], vs[:, :, H:H + 2].rearrange("p c o -> p o c")).then_inc(own, 1)

            @block.sync
            def _(sp):
                sp.wait_ge(own, 1)
                sp.dma_start(key_cols.rearrange("o (p c) -> p o c", c=EC), compact[:, :, :]).then_inc(sent, 16)
                sp.wait_ge(sent, 16)
        with ExitStack() as ctx:
            sbo = sb_in(ctx, "ss_")
            spread = sbo("spread", [P, EC, 2 * H])
            with ExitStack() as c2:
                s_in = sem_in(c2, "ss_")("s_in")
                block = c2.enter_context(nc.Block())

                @block.sync
                def _(sp):
                    sp.dma_start(spread[:, :, :], starts_s.rearrange("(p c) h -> p c h", c=EC)).then_inc(s_in, 16)
                    sp.wait_ge(s_in, 16)
            scan_runs("ssx_", fs, spread, 2 * H, "sum")
            with ExitStack() as c2:
                sb, sem = sb_in(c2, "se_"), sem_in(c2, "se_")
                own = sem("own")
                block = c2.enter_context(nc.Block())

                @block.vector
                def _(dve):
                    link = chain(dve, own)
                    nc.vector.tensor_copy(rows[:, :, H:2 * H], spread[:, :, 0:H])
                    link(nc.vector.tensor_tensor(vs[:, :, 0:H], vs[:, :, 0:H], spread[:, :, H:2 * H], ALU.add))
                    link(nc.vector.tensor_scalar(spread[:, :, 0:H], vs[:, :, 0:H], SLOPE, None, ALU.mult))
                    link(nc.vector.tensor_tensor(rows[:, :, 2 * H:3 * H], vs[:, :, 0:H], spread[:, :, 0:H], ALU.max))
        with ExitStack() as ctx:
            softmax_runs("sm_", fs, rows[:, :, 2 * H:3 * H], rows[:, :, 0:H], ctx)
        with ExitStack() as ctx:
            sent = sem_in(ctx, "so_")("sent")
            block = ctx.enter_context(nc.Block())

            @block.sync
            def _(sp):
                sp.dma_start(from_src.rearrange("(p c) h -> p c h", c=EC), rows[:, :, :]).then_inc(sent, 16)
                sp.wait_ge(sent, 16)

    def gather_rows(got, pos, from_src):
        with ExitStack() as ctx:
            sb, sem = sb_in(ctx, "gt_"), sem_in(ctx, "gt_")
            ring = sb("ring", [P, 2, G, 3 * H])
            index = sb("index", [P, 2, G], I32)
            staged, landed, taken, gate = sem("staged"), [sem("landed0"), sem("landed1")], sem("taken"), sem("gate")
            block = ctx.enter_context(nc.Block())

            @block.scalar
            def _(act):
                for u in range(2):
                    nc.scalar.activation(index[:, u, :], pos[:, u * G:(u + 1) * G], ACT.Copy).then_inc(staged, 1)
                with act.Fori(1, NB // 2) as b:
                    for u in range(2):
                        act.wait_ge(landed[u], b * (16 * G))
                        nc.scalar.activation(index[:, u, :], pos[:, bass.ds((2 * b + u) * G, G)], ACT.Copy).then_inc(staged, 1)

            @block.gpsimd
            def _(pool):
                with pool.Fori(0, NB // 2) as b:
                    for u in range(2):
                        pool.wait_ge(staged, 2 * b + u + 1)
                        pool.wait_ge(taken, 2 * b + u + 1)
                        pool.sem_inc(gate, 1)
                        for g in range(G):
                            pool.indirect_dma_start(ring[:, u, g, :], None, from_src,
                                                    bass.IndirectOffsetOnAxis(ap=index[:, u, g:g + 1].bitcast(U32), axis=0)).then_inc(landed[u], 16)

            @block.vector
            def _(dve):
                dve.sem_inc(taken, 2)
                with dve.Fori(0, NB // 2) as b:
                    for u in range(2):
                        dve.wait_ge(landed[u], b * (16 * G) + 16 * G)
                        nc.vector.tensor_copy(got[:, bass.ds((2 * b + u) * G, G), :], ring[:, u, :, :]).then_inc(taken, 1)
                dve.wait_ge(taken, NB + 2)

    def target_softmax(fd, got, sums_d, base_d, deg_d, msg):
        with ExitStack() as ctx:
            a_dst = sb_in(ctx, "td_")("a_dst", [P, EC, H])
            with ExitStack() as c2:
                softmax_runs("tm_", fd, got[:, :, 2 * H:3 * H], a_dst[:, :, :], c2)
            with ExitStack() as c2:
                sem = sem_in(c2, "ta_")
                prod, root, own = sem("prod"), sem("root"), sem("own")
                block = c2.enter_context(nc.Block())

                @block.vector
                def _(dve):
                    nc.vector.tensor_tensor(a_dst[:, :, :], a_dst[:, :, :], got[:, :, 0:H], ALU.mult).then_inc(prod, 1)
                    dve.wait_ge(root, 1)
                    nc.vector.tensor_tensor(a_dst[:, :, :], a_dst[:, :, :], got[:, :, H:2 * H], ALU.mult).then_inc(own, 1)
                    dve.wait_ge(own, 1)

                @block.scalar
                def _(act):
                    act.wait_ge(prod, 1)
                    nc.scalar.activation(a_dst[:, :, :], a_dst[:, :, :], ACT.Sqrt).then_inc(root, 1)
            scan_runs("tsum_", fd, a_dst, H, "sum")
            with ExitStack() as c2:
                sb, sem = sb_in(c2, "tg_"), sem_in(c2, "tg_")
                lastf, has = sb("lastf", [P, NJ]), sb("has", [P, NJ])
                last_i = sb("last_i", [P, NJ], I32)
                own, index_ready, sums_out, landed = sem("own"), sem("index_ready"), sem("sums_out"), sem("landed")
                block = c2.enter_context(nc.Block())

                @block.sync
                def _(sp):
                    sp.dma_start(sums_d.rearrange("(p c) h -> p c h", c=EC), a_dst[:, :, :]).then_inc(sums_out, 16)

                @block.vector
                def _(dve):
                    link = chain(dve, own)
                    link(nc.vector.tensor_tensor(lastf[:, :], base_d[:, :], deg_d[:, :], ALU.add))
                    link(nc.vector.tensor_scalar(lastf[:, :], lastf[:, :], 1.0, 0.0, ALU.subtract, ALU.max))
                    nc.vector.tensor_scalar(has[:, :], deg_d[:, :], 0.0, None, ALU.is_gt)
                    nc.vector.tensor_copy(last_i[:, :], lastf[:, :]).then_inc(index_ready, 1)
                    dve.wait_ge(landed, 16 * NJ)
                    link(nc.vector.tensor_tensor(msg[:, :, :], msg[:, :, :], has[:, :].unsqueeze(2).to_broadcast([P, NJ, H]), ALU.mult))

                @block.gpsimd
                def _(pool):
                    pool.wait_ge(index_ready, 1)
                    pool.wait_ge(sums_out, 16)
                    for j in range(NJ):
                        pool.indirect_dma_start(msg[:, j, :], None, sums_d,
                                                bass.IndirectOffsetOnAxis(ap=last_i[:, j:j + 1].bitcast(U32), axis=0)).then_inc(landed, 16)

    def degrees(deg_d):
        with ExitStack() as ctx:
            sem = sem_in(ctx, "dg_")
            own, root = sem("own"), sem("root")
            block = ctx.enter_context(nc.Block())

            @block.vector
            def _(dve):
                link = chain(dve, own)
                link(nc.vector.tensor_scalar(dinv[:, :], deg_d[:, :], 1.0, None, ALU.add))
                dve.wait_ge(root, 1)
                link(nc.vector.reciprocal(dinv[:, :], dinv[:, :]))

            @block.scalar
            def _(act):
                act.wait_ge(own, 1)
                nc.scalar.activation(dinv[:, :], dinv[:, :], ACT.Sqrt).then_inc(root, 1)

    def apply_nodes(msg):
        with ExitStack() as outer:
            sbo = sb_in(outer, "ap_")
            hT = sbo("hT", [H, NJ, P])
            with ExitStack() as ctx:
                sb, sem = sb_in(ctx, "bn_"), sem_in(ctx, "bn_")
                part, total, scale = sb("part", [P, H]), sb("total", [P, H]), sb("scale", [P, H])
                gamma, beta, sq = sb("gamma", [P, H]), sb("beta", [P, H]), sb("sq", [P, NJ, H])
                own, gb_in, part_ready, summed = sem("own"), sem("gb_in"), sem("part_ready"), sem("summed")
                var_ready, dev_ready, h_ready, turned = sem("var_ready"), sem("dev_ready"), sem("h_ready"), sem("turned")
                block = ctx.enter_context(nc.Block())

                @block.sync
                def _(sp):
                    sp.dma_start(gamma[:, :], a["L0_gnn_bn_gamma"].unsqueeze(0).to_broadcast([P, H])).then_inc(gb_in, 16)
                    sp.dma_start(beta[:, :], a["L0_gnn_bn_beta"].unsqueeze(0).to_broadcast([P, H])).then_inc(gb_in, 16)

                @block.tensor
                def _(pe):
                    for n in range(2):
                        pe.wait_ge(part_ready, n + 1)
                        nc.tensor.matmul(ps[n][0:P, 0:H], ones[:, 0:P], part[:, :], start=True, stop=True).then_inc(summed, 1)
                    pe.wait_ge(h_ready, 1)
                    for j in range(NJ):
                        t = nc.tensor.transpose(ps[j // 4][0:H, j % 4 * P:(j % 4 + 1) * P], msg[:, j, :], ident[0:P, 0:P])
                    t.then_inc(turned, 1)

                @block.scalar
                def _(act):
                    act.wait_ge(var_ready, 1)
                    nc.scalar.activation(scale[:, :], scale[:, :], ACT.Sqrt).then_inc(dev_ready, 1)

                @block.vector
                def _(dve):
                    link = chain(dve, own)
                    over_j = lambda t: t[:, :, :].rearrange("p j h -> p h j")
                    wide = lambda t: t[:, :].unsqueeze(1).to_broadcast([P, NJ, H])
                    nc.vector.tensor_reduce(part[:, :], over_j(msg), AX.X, ALU.add).then_inc(part_ready, 1)
                    dve.wait_ge(summed, 1)
                    link(nc.vector.tensor_scalar(total[:, :], ps[0][0:P, 0:H], 1.0 / N, None, ALU.mult))
                    link(nc.vector.tensor_tensor(msg[:, :, :], msg[:, :, :], wide(total), ALU.subtract))
                    link(nc.vector.tensor_tensor(sq[:, :, :], msg[:, :, :], msg[:, :, :], ALU.mult))
                    nc.vector.tensor_reduce(part[:, :], over_j(sq), AX.X, ALU.add).then_inc(part_ready, 1)
                    dve.wait_ge(summed, 2)
                    nc.vector.tensor_scalar(scale[:, :], ps[1][0:P, 0:H], 1.0 / N, BN_EPS, ALU.mult, ALU.add).then_inc(var_ready, 1)
                    dve.wait_ge(dev_ready, 1)
                    link(nc.vector.reciprocal(scale[:, :], scale[:, :]))
                    dve.wait_ge(gb_in, 32)
                    link(nc.vector.tensor_tensor(scale[:, :], scale[:, :], gamma[:, :], ALU.mult))
                    link(nc.vector.tensor_tensor(msg[:, :, :], msg[:, :, :], wide(scale), ALU.mult))
                    nc.vector.tensor_tensor(msg[:, :, :], msg[:, :, :], wide(beta), ALU.add).then_inc(h_ready, 1)
                    dve.wait_ge(turned, 1)
                    for c in range(0, NJ, 4):
                        m = min(4, NJ - c)
                        last = nc.vector.tensor_copy(hT[:, c:c + m, :], ps[c // 4][0:H, 0:m * P].rearrange("h (j p) -> h j p", p=P))
                    link(last)
            with ExitStack() as ctx:
                sb, sem = sb_in(ctx, "aw_"), sem_in(ctx, "aw_")
                wd, wa, wg = sb("wd", [128, KD, D]), sb("wa", [128, KD, D]), sb("wg", [H, D])
                rT = sb("rT", [128, KD, NJ, P])
                t = sb("t", [128, 2, 4 * P])
                bias, bias2, brow = sb("bias", [128, KD]), sb("bias2", [128, KD]), sb("brow", [1, D])
                w_in, up, taken, low, down, added = sem("w_in"), sem("up"), sem("taken"), sem("low"), sem("down"), sem("added")
                own = sem("own")
                block = ctx.enter_context(nc.Block())
                chunks = [(o, c, min(4, NJ - c)) for c in range(0, NJ, 4) for o in range(KD)]

                @block.sync
                def _(sp):
                    sp.dma_start(wd[:, :, :], a["L0_gnn_W_apply_dst"].rearrange("(k q) d -> q k d", k=KD)).then_inc(w_in, 16)
                    sp.dma_start(wa[:, :, :], a["L0_gnn_W_apply"].rearrange("(k q) d -> q k d", k=KD)).then_inc(w_in, 16)
                    sp.dma_start(wg[:, :], a["L0_gnn_W_agg"]).then_inc(w_in, 16)
                    for k in range(KD):
                        half = slice(k * 128, (k + 1) * 128)
                        sp.dma_start(bias[:, k:k + 1], a["L0_gnn_b_agg"][half].unsqueeze(1)).then_inc(w_in, 16)
                        sp.dma_start(bias2[:, k:k + 1], a["L0_gnn_b_apply_dst"][half].unsqueeze(1)).then_inc(w_in, 16)
                    sp.dma_start(brow[:, :], a["L0_gnn_b_apply"].unsqueeze(0)).then_inc(w_in, 16)

                @block.tensor
                def _(pe):
                    pe.wait_ge(w_in, 8 * 16)
                    for i, (o, c, m) in enumerate(chunks):
                        if i >= 4:
                            pe.wait_ge(taken, i - 3)
                        cols = slice(o * 128, (o + 1) * 128)
                        for k in range(KD):
                            nc.tensor.matmul(ps[i % 4][:, 0:m * P], wd[:, k, cols], xnT[:, k, c:c + m, :].rearrange("q j p -> q (j p)"),
                                             start=k == 0, stop=False)
                        nc.tensor.matmul(ps[i % 4][:, 0:m * P], wg[:, cols], hT[:, c:c + m, :].rearrange("q j p -> q (j p)"),
                                         start=False, stop=True).then_inc(up, 1)
                    for j in range(NJ):
                        pe.wait_ge(low, 2 * (j // 4) + 2)
                        if j >= 4:
                            pe.wait_ge(added, j - 3)
                        for k in range(KD):
                            nc.tensor.matmul(ps[4 + j % 4][0:P, 0:D], rT[:, k, j, :], wa[:, k, :], start=k == 0, stop=False)
                        nc.tensor.matmul(ps[4 + j % 4][0:P, 0:D], ones[0:1, 0:P], brow[:, :], start=False, stop=True).then_inc(down, 1)

                @block.vector
                def _(dve):
                    dve.wait_ge(w_in, 8 * 16)
                    nc.vector.tensor_tensor(bias[:, :], bias[:, :], bias2[:, :], ALU.add).then_inc(own, 1)
                    dve.wait_ge(own, 1)
                    for i, (o, c, m) in enumerate(chunks):
                        dve.wait_ge(up, i + 1)
                        nc.vector.tensor_scalar(t[:, i % 2, 0:m * P], ps[i % 4][:, 0:m * P], bias[:, o:o + 1], None, ALU.add).then_inc(taken, 1)
                        dve.wait_ge(taken, i + 1)
                        nc.vector.scalar_tensor_tensor(out=rT[:, o, c:c + m, :].rearrange("q j p -> q (j p)"), in0=t[:, i % 2, 0:m * P],
                                                       scalar=SLOPE, in1=t[:, i % 2, 0:m * P], op0=ALU.mult, op1=ALU.max).then_inc(low, 1)
                    for j in range(NJ):
                        dve.wait_ge(down, j + 1)
                        nc.vector.tensor_tensor(x[:, j, :], x[:, j, :], ps[4 + j % 4][0:P, 0:D], ALU.add).then_inc(added, 1)
                    dve.wait_ge(added, NJ)


    def layer0_ffn():
        CT = 5
        HT = X0F // 128
        halves = ((0, 3), (3, 5))
        with ExitStack() as outer:
            sbo = sb_in(outer, "f0_")
            comb = sbo("comb", [P, NJ, NEXP])
            w1 = sbo("w1", [128, NEXP, KD, X0F])
            w2 = sbo("w2", [128, NEXP, HT, D])
            b1 = sbo("b1", [128, NEXP, HT])
            sem0 = sem_in(outer, "f0_")
            weights_in = sem0("weights_in")
            with ExitStack() as ctx:
                sb, sem = sb_in(ctx, "g0_"), sem_in(ctx, "g0_")
                wg = sb("wg", [128, KD, NEXP])
                bg, bias = sb("bg", [P, NEXP]), sb("bias", [P, NEXP])
                lg = sb("lg", [P, NJ, NEXP])
                top8 = sb("top8", [P, NJ, 8])
                idx8 = sb("idx8", [P, NJ, 8], U32)
                idxf, expo, hit, hit2 = sb("idxf", [P, NJ, 2]), sb("expo", [P, NJ, 2]), sb("hit", [P, NJ, NEXP]), sb("hit2", [P, NJ, NEXP])
                iota_i, iota = sb("iota_i", [P, NEXP], I32), sb("iota", [P, NEXP])
                b2, combT = sb("b2", [NEXP, D]), sb("combT", [NEXP, NJ, P])
                g_in, made, gated, own = sem("g_in"), sem("made"), sem("gated"), sem("own")
                less, exps, comb_ready, turned, kept = sem("less"), sem("exps"), sem("comb_ready"), sem("turned"), sem("kept")
                biased, added = sem("biased"), sem("added")
                block = ctx.enter_context(nc.Block())

                @block.sync
                def _(sp):
                    sp.dma_start(wg[:, :, :], a["L0_ffn_Wg"].rearrange("(k q) e -> q k e", k=KD)).then_inc(g_in, 16)
                    sp.dma_start(bg[:, :], a["L0_ffn_bg"].unsqueeze(0).to_broadcast([P, NEXP])).then_inc(g_in, 16)
                    sp.dma_start(bias[:, :], a["L0_ffn_bias"].unsqueeze(0).to_broadcast([P, NEXP])).then_inc(g_in, 16)
                    sp.dma_start(b2[:, :], a["L0_ffn_b2"]).then_inc(g_in, 16)
                    sp.dma_start(w1[:, :, :, :].rearrange("q e k h -> q (e k) h"), a["L0_ffn_W1"].rearrange("e (k q) h -> q (e k) h", k=KD)).then_inc(weights_in, 16)
                    sp.dma_start(w2[:, :, :, :].rearrange("q e m d -> q (e m) d"), a["L0_ffn_W2"].rearrange("e (m q) d -> q (e m) d", m=HT)).then_inc(weights_in, 16)
                    sp.dma_start(b1[:, :, :].rearrange("q e m -> q (e m)"), a["b1_0_cols"]).then_inc(weights_in, 16)

                @block.gpsimd
                def _(pool):
                    pool.iota(iota_i[:, :], [[1, NEXP]], base=0, channel_multiplier=0).then_inc(made, 1)

                @block.tensor
                def _(pe):
                    pe.wait_ge(g_in, 64)
                    for j in range(NJ):
                        for k in range(KD):
                            m = nc.tensor.matmul(ps[0][0:P, j * NEXP:(j + 1) * NEXP], xnT[:, k, j, :], wg[:, k, :],
                                                 start=k == 0, stop=k == KD - 1)
                    m.then_inc(gated, 1)
                    pe.wait_ge(comb_ready, 1)
                    for j in range(NJ):
                        t = nc.tensor.transpose(ps[1 + j // 4][0:NEXP, j % 4 * P:(j % 4 + 1) * P], comb[:, j, :], ident[0:P, 0:P])
                    t.then_inc(turned, 1)
                    pe.wait_ge(kept, 1)
                    for j in range(NJ):
                        if j >= 8:
                            pe.wait_ge(added, j - 7)
                        nc.tensor.matmul(ps[j % 8][0:P, 0:D], combT[:, j, :], b2[:, :], start=True, stop=True).then_inc(biased, 1)

                @block.scalar
                def _(act):
                    act.wait_ge(less, 1)
                    nc.scalar.activation(expo[:, :, 1], expo[:, :, 0], ACT.Exp).then_inc(exps, 1)

                @block.vector
                def _(dve):
                    link = chain(dve, own)
                    wide = lambda t: t[:, :].unsqueeze(1).to_broadcast([P, NJ, NEXP])
                    each = lambda t: t.unsqueeze(2).to_broadcast([P, NJ, NEXP])
                    dve.wait_ge(g_in, 64)
                    dve.wait_ge(gated, 1)
                    link(nc.vector.tensor_tensor(lg[:, :, :], ps[0][0:P, 0:NJ * NEXP].rearrange("p (j e) -> p j e", e=NEXP), wide(bg), ALU.add))
                    link(nc.vector.tensor_tensor(lg[:, :, :], lg[:, :, :], wide(bias), ALU.add))
                    for j in range(NJ):
                        last = nc.vector.max(top8[:, j, :], lg[:, j, :])
                    link(last)
                    for j in range(NJ):
                        last = nc.vector.max_index(idx8[:, j, :], top8[:, j, :], lg[:, j, :])
                    link(last)
                    nc.vector.tensor_tensor(expo[:, :, 0], top8[:, :, 1], top8[:, :, 0], ALU.subtract).then_inc(less, 1)
                    dve.wait_ge(made, 1)
                    nc.vector.tensor_copy(iota[:, :], iota_i[:, :])
                    link(nc.vector.tensor_copy(idxf[:, :, :], idx8[:, :, 0:2]))
                    dve.wait_ge(exps, 1)
                    link(nc.vector.tensor_scalar(expo[:, :, 0], expo[:, :, 1], 1.0, None, ALU.add))
                    link(nc.vector.reciprocal(expo[:, :, 0], expo[:, :, 0]))
                    link(nc.vector.tensor_tensor(expo[:, :, 1], expo[:, :, 1], expo[:, :, 0], ALU.mult))
                    for n, h in enumerate((hit, hit2)):
                        link(nc.vector.tensor_tensor(h[:, :, :], wide(iota), each(idxf[:, :, n]), ALU.is_equal))
                        link(nc.vector.tensor_tensor(h[:, :, :], h[:, :, :], each(expo[:, :, n]), ALU.mult))
                    nc.vector.tensor_tensor(comb[:, :, :], hit[:, :, :], hit2[:, :, :], ALU.add).then_inc(comb_ready, 1)
                    dve.wait_ge(turned, 1)
                    for c in range(0, NJ, 4):
                        m = min(4, NJ - c)
                        last = nc.vector.tensor_copy(combT[:, c:c + m, :], ps[1 + c // 4][0:NEXP, 0:m * P].rearrange("h (j p) -> h j p", p=P))
                    last.then_inc(kept, 1)
                    for j in range(NJ):
                        dve.wait_ge(biased, j + 1)
                        nc.vector.tensor_tensor(x[:, j, :], x[:, j, :], ps[j % 8][0:P, 0:D], ALU.add).then_inc(added, 1)
                    dve.wait_ge(added, NJ)
            with ExitStack() as ctx:
                sb, sem = sb_in(ctx, "e0_"), sem_in(ctx, "e0_")
                hT = sb("hT", [128, 2, HT, CT * P])
                up, relued, down, added = sem("up"), sem("relued"), sem("down"), sem("added")
                block = ctx.enter_context(nc.Block())
                UPS, DOWNS = NEXP * HT * 2, NEXP * CT

                @block.tensor
                def _(pe):
                    pe.wait_ge(weights_in, 48)
                    pe.sem_inc(down, 2 * CT)

                    def rise(b, e):
                        for m in range(HT):
                            for f, (lo, hi) in enumerate(halves):
                                i = (e * HT + m) * 2 + f
                                pe.wait_ge(relued, b * UPS + i + 1)
                                for k in range(KD):
                                    last = nc.tensor.matmul(ps[i % 4][:, 0:(hi - lo) * P], w1[:, e, k, m * 128:(m + 1) * 128],
                                                            xnT[:, k, bass.ds(b * CT + lo, hi - lo), :].rearrange("q j p -> q (j p)"),
                                                            start=k == 0, stop=k == KD - 1)
                                last.then_inc(up, 1)

                    def fall(b, e):
                        pe.wait_ge(relued, b * UPS + (e + 1) * HT * 2 + 4)
                        for t in range(CT):
                            i = e * CT + t
                            pe.wait_ge(added, b * DOWNS + i + 1)
                            for m in range(HT):
                                last = nc.tensor.matmul(ps[4 + i % 4][0:P, 0:D], hT[:, e % 2, m, t * P:(t + 1) * P], w2[:, e, m, :],
                                                        start=m == 0, stop=m == HT - 1)
                            last.then_inc(down, 1)

                    with pe.Fori(0, NJ // CT) as b:
                        rise(b, 0)
                        for e in range(NEXP):
                            if e + 1 < NEXP:
                                rise(b, e + 1)
                            fall(b, e)

                @block.scalar
                def _(act):
                    act.wait_ge(weights_in, 48)
                    act.sem_inc(relued, 4)
                    with act.Fori(0, NJ // CT) as b:
                        for e in range(NEXP):
                            act.wait_ge(down, b * DOWNS + (e + 1) * CT)
                            for m in range(HT):
                                for f, (lo, hi) in enumerate(halves):
                                    i = (e * HT + m) * 2 + f
                                    act.wait_ge(up, b * UPS + i + 1)
                                    nc.scalar.activation(hT[:, e % 2, m, lo * P:hi * P], ps[i % 4][:, 0:(hi - lo) * P], ACT.Relu,
                                                         bias=b1[:, e, m:m + 1]).then_inc(relued, 1)

                @block.vector
                def _(dve):
                    dve.sem_inc(added, 4)
                    with dve.Fori(0, NJ // CT) as b:
                        for e in range(NEXP):
                            for t in range(CT):
                                i = e * CT + t
                                dve.wait_ge(down, b * DOWNS + i + 1 + 2 * CT)
                                dve.wait_ge(added, b * DOWNS + i + 1)
                                row = x[:, bass.ds(b * CT + t, 1), :].rearrange("p a d -> p (a d)")
                                nc.vector.scalar_tensor_tensor(out=row, in0=ps[4 + i % 4][0:P, 0:D],
                                                               scalar=comb[:, bass.ds(b * CT + t, 1), e:e + 1].rearrange("p a e -> p (a e)"),
                                                               in1=row, op0=ALU.mult, op1=ALU.add).then_inc(added, 1)
                    dve.wait_ge(added, NJ // CT * DOWNS + 4)

    EB = 4 * P
    MID = N // 2
    PAIRS = EC // 2
    adjacency = dram("adjacency", (NJ, P, N), F16)

    def build_adjacency():
        with ExitStack() as outer:
            sbo = sb_in(outer, "ba_")
            key_t = sbo("key_t", [P, 2, EC])
            nodes_row = sbo("nodes_row", [P, N], F16)
            bounds = sbo("bounds", [1, 3, NJ], I32)
            ident_b, zero_b = sbo("ident_b", [P, P], F16), sbo("zero_b", [P, EB], F16)
            with ExitStack() as ctx:
                sb, sem = sb_in(ctx, "bp_"), sem_in(ctx, "bp_")
                tiles = sb("tiles", [100, 2, 4, P])
                nodes_i = sb("nodes_i", [P, N], I32)
                b3, cum = sb("b3", [1, 3, NJ]), sb("cum", [1, NJ])
                keys_in, made, turned, own, floor_ready = sem("keys_in"), sem("made"), sem("turned"), sem("own"), sem("floor_ready")
                block = ctx.enter_context(nc.Block())

                @block.sync
                def _(sp):
                    for o in range(2):
                        sp.dma_start(tiles[:, o, :, :], key_cols[o].rearrange("(a k i) -> k a i", a=4, i=P)).then_inc(keys_in, 16)

                @block.gpsimd
                def _(pool):
                    pool.iota(nodes_i[:, :], [[1, N]], base=0, channel_multiplier=0).then_inc(made, 1)

                @block.tensor
                def _(pe):
                    pe.wait_ge(keys_in, 32)
                    for o in range(2):
                        for q in range(4):
                            t = nc.tensor.transpose(ps[o][0:P, q * 100:(q + 1) * 100], tiles[:, o, q, :], ident[0:100, 0:100])
                        t.then_inc(turned, 1)

                @block.vector
                def _(dve):
                    link = chain(dve, own)
                    nc.vector.memset(zero_b[:, :], 0.0)
                    nc.vector.tensor_copy(ident_b[:, :], ident[0:P, 0:P])
                    w = window[0:1, :]
                    link(nc.vector.tensor_scalar(b3[:, 0, :], w[:, 0:NJ], 1.0 / (2 * P), -0.498, ALU.mult, ALU.add))
                    link(nc.vector.tensor_scalar(b3[:, 0, :], b3[:, 0, :], ROUND, ROUND, ALU.add, ALU.subtract))
                    link(nc.vector.tensor_scalar(b3[:, 0, :], b3[:, 0, :], float(PAIRS - 2), None, ALU.min))
                    link(nc.vector.tensor_scalar(b3[:, 1, :], w[:, 1:NJ + 1], 1.0 / (2 * P), 0.498, ALU.mult, ALU.add))
                    link(nc.vector.tensor_scalar(b3[:, 1, :], b3[:, 1, :], ROUND, ROUND, ALU.add, ALU.subtract))
                    link(nc.vector.tensor_scalar(cum[:, :], b3[:, 0, :], 2.0, None, ALU.add))
                    link(nc.vector.tensor_tensor(b3[:, 1, :], b3[:, 1, :], cum[:, :], ALU.max))
                    link(nc.vector.tensor_tensor(b3[:, 2, :], b3[:, 1, :], b3[:, 0, :], ALU.subtract))
                    link(nc.vector.tensor_tensor_scan(cum[:, :], ones[0:1, 0:NJ], b3[:, 2, :], 0.0, ALU.mult, ALU.add))
                    link(nc.vector.tensor_tensor(cum[:, :], cum[:, :], b3[:, 1, :], ALU.subtract))
                    link(nc.vector.tensor_copy(b3[:, 2, :], cum[:, :]))
                    nc.vector.tensor_copy(bounds[:, :, :], b3[:, :, :])
                    dve.wait_ge(made, 1)
                    nc.vector.tensor_scalar(nodes_row[:, :], nodes_i[:, :], float(MID), None, ALU.subtract)
                    for o in range(2):
                        dve.wait_ge(turned, o + 1)
                        last = nc.vector.tensor_scalar(key_t[:, o, :], ps[o][0:P, 0:EC], float(MID), None, ALU.subtract)
                    link(last)
            with ExitStack() as ctx:
                sb, sem = sb_in(ctx, "bb_"), sem_in(ctx, "bb_")
                hot_s, hot_d = sb("hot_s", [P, 2, P], F16), sb("hot_d", [P, 2, N], F16)
                rows = sb("rows", [P, 2, N], F16)
                hot_ready, used, window_done = sem("hot_ready"), sem("used"), sem("window_done")
                kept_a, kept_v, sent = sem("kept_a"), sem("kept_v"), [sem("sent0"), sem("sent1")]
                NBK = -(-N // EB)
                ACT_BANKS = 4
                block = ctx.enter_context(nc.Block())
                bank_cols = [(i * EB, min((i + 1) * EB, N)) for i in range(NBK)]

                def limits(eng, j):
                    top_ = {0: PAIRS - 2, 1: PAIRS, 2: 2 * PAIRS + 2 * NJ}
                    return [eng.value_load(bounds[0:1, i, j:j + 1], min_val=0, max_val=top_[i]) for i in range(3)]

                @block.vector
                def _(dve):
                    dve.sem_inc(used, 2)
                    for j in range(NJ):
                        first, end, off = limits(dve, j)
                        with dve.Fori(first, end) as kk:
                            for u in range(2):
                                dve.wait_ge(used, (kk + off) * 2 + u + 1)
                                nc.vector.tensor_scalar(hot_s[:, u, :], nodes_row[:, j * P:(j + 1) * P], key_t[:, 0, bass.ds(kk * 2 + u, 1)],
                                                        None, ALU.is_equal)
                                nc.vector.tensor_scalar(hot_d[:, u, :], nodes_row[:, :], key_t[:, 1, bass.ds(kk * 2 + u, 1)],
                                                        None, ALU.is_equal).then_inc(hot_ready, 1)
                        dve.wait_ge(window_done, j + 1)
                        if j >= 2:
                            dve.wait_ge(sent[j % 2], 16 * (j // 2))
                        for i, (lo, hi) in list(enumerate(bank_cols))[ACT_BANKS:]:
                            nc.vector.tensor_copy(rows[:, j % 2, lo:hi], ps[i][0:P, 0:hi - lo]).then_inc(kept_v, 1)

                @block.tensor
                def _(pe):
                    def pair(kk, off, start):
                        for u in range(2):
                            pe.wait_ge(hot_ready, (kk + off) * 2 + u + 1)
                            for i, (lo, hi) in enumerate(bank_cols):
                                m = nc.tensor.matmul(ps[i][0:P, 0:hi - lo], hot_s[:, u, :], hot_d[:, u, lo:hi],
                                                     start=start and u == 0, stop=False)
                            m.then_inc(used, 1)

                    for j in range(NJ):
                        first, end, off = limits(pe, j)
                        if j:
                            pe.wait_ge(kept_a, ACT_BANKS * j)
                            pe.wait_ge(kept_v, (NBK - ACT_BANKS) * j)
                        pair(first, off, True)
                        with pe.Fori(first + 1, end) as kk:
                            pair(kk, off, False)
                        at = (j % 4) * P
                        nc.tensor.matmul(ps[j // 4][0:P, at:at + P], ident_b[:, :], ident_b[:, :], start=False, stop=False)
                        for i, (lo, hi) in enumerate(bank_cols):
                            m = nc.tensor.matmul(ps[i][0:P, 0:hi - lo], zero_b[:, 0:P], zero_b[:, 0:hi - lo], start=False, stop=True)
                        m.then_inc(window_done, 1)

                @block.scalar
                def _(act):
                    for j in range(NJ):
                        act.wait_ge(window_done, j + 1)
                        if j >= 2:
                            act.wait_ge(sent[j % 2], 16 * (j // 2))
                        for i, (lo, hi) in list(enumerate(bank_cols))[:ACT_BANKS]:
                            nc.scalar.activation(rows[:, j % 2, lo:hi], ps[i][0:P, 0:hi - lo], ACT.Copy).then_inc(kept_a, 1)

                @block.sync
                def _(sp):
                    for j in range(NJ):
                        sp.wait_ge(kept_a, ACT_BANKS * (j + 1))
                        sp.wait_ge(kept_v, (NBK - ACT_BANKS) * (j + 1))
                        sp.dma_start(adjacency[j], rows[:, j % 2, :]).then_inc(sent[j % 2], 16)
                    for u in range(2):
                        sp.wait_ge(sent[u], 16 * ((NJ + 1 - u) // 2))

    PARTS = 2
    TOP = 16384.0
    SLOTS = 5
    PASSES = ((0, 16), (16, NJ))

    def convolve(tag, w_name, b_name, last_layer):
        with ExitStack() as ctx:
            sb, sem = sb_in(ctx, tag), sem_in(ctx, tag)
            w, bias = sb("w", [128, KD, D]), sb("bias", [P, D])
            h = sb("h", [P, NJ, D])
            big = sb("big", [P, NJ])
            big1, scale, back, out_scale = sb("big1", [P, 1]), sb("scale", [P, 1]), sb("back", [P, 1]), sb("out_scale", [P, NJ])
            bigT = sb("bigT", [1, 2])
            parts = sb("parts", [P, NJ, PARTS, D], F16)
            y = sb("y", [P, NJ, D])
            stream = sb("stream", [P, SLOTS, 16 * P], F16)
            w_in, mult, hs, split, own = sem("w_in"), sem("mult"), sem("hs"), sem("split"), sem("own")
            highs, big_ready, big_turned, top_ready, top_spread, scaled = (
                sem(n) for n in ("highs", "big_ready", "big_turned", "top_ready", "top_spread", "scaled"))
            landed = [sem(f"landed{u}") for u in range(SLOTS)]
            used, summed, taken, active, turned, kept = (sem(n) for n in ("used", "summed", "taken", "active", "turned", "kept"))
            block = ctx.enter_context(nc.Block())

            @block.sync
            def _(sp):
                sp.dma_start(w[:, :, :], a[w_name].rearrange("(k q) d -> q k d", k=KD)).then_inc(w_in, 16)
                sp.dma_start(bias[:, :], a[b_name].unsqueeze(0).to_broadcast([P, D])).then_inc(w_in, 16)
                for n, (lo, hi) in enumerate(PASSES):
                    for j in range(NJ):
                        i = n * NJ + j
                        if i >= SLOTS:
                            sp.wait_ge(used, i - SLOTS + 1)
                        sp.dma_start(stream[:, i % SLOTS, 0:(hi - lo) * P], adjacency[j][:, lo * P:hi * P]).then_inc(landed[i % SLOTS], 16)

            @block.tensor
            def _(pe):
                pe.wait_ge(w_in, 32)
                for j in range(NJ):
                    if j >= 8:
                        pe.wait_ge(hs, j - 7)
                    for k in range(KD):
                        m = nc.tensor.matmul(ps[j % 8][0:P, 0:D], xnT[:, k, j, :], w[:, k, :], start=k == 0, stop=k == KD - 1)
                    m.then_inc(mult, 1)
                pe.wait_ge(big_ready, 1)
                nc.tensor.transpose(ps[0][0:1, 0:P], big1[:, :], ident[0:P, 0:P]).then_inc(big_turned, 1)
                pe.wait_ge(top_ready, 1)
                nc.tensor.matmul(ps[1][0:P, 0:2], ones[0:1, 0:P], bigT[:, :], start=True, stop=True).then_inc(top_spread, 1)
                pe.wait_ge(scaled, 1)

                def source_row(n, lo, hi, it, u, start, stop):
                    pe.wait_ge(landed[u], (it + n * (NJ // SLOTS)) * 16 + 16)
                    j = it * SLOTS + u
                    for jd in range(lo, hi):
                        i = jd - lo
                        for part in range(PARTS):
                            m = nc.tensor.matmul(ps[i // 2][0:P, i % 2 * D:(i % 2 + 1) * D], stream[:, u, i * P:(i + 1) * P],
                                                 parts[:, bass.ds(j, 1), part, :].rearrange("p a d -> p (a d)"),
                                                 start=start and part == 0 and i % 2 == 0,
                                                 stop=stop and part == PARTS - 1 and (i % 2 == 1 or jd == hi - 1))
                    m.then_inc(used, 1)
                    return m

                for n, (lo, hi) in enumerate(PASSES):
                    if n:
                        pe.wait_ge(taken, lo)
                    for u in range(SLOTS):
                        if n == 0:
                            pe.wait_ge(split, u + 1)
                        source_row(n, lo, hi, 0, u, u == 0, False)
                    if n == 0:
                        pe.wait_ge(split, NJ)
                    with pe.Fori(1, NJ // SLOTS - 1) as it:
                        for u in range(SLOTS):
                            source_row(n, lo, hi, it, u, False, False)
                    for u in range(SLOTS):
                        m = source_row(n, lo, hi, NJ // SLOTS - 1, u, False, u == SLOTS - 1)
                if not last_layer:
                    pe.wait_ge(taken, NJ)
                    for j in range(NJ):
                        pe.wait_ge(active, j + 1)
                        if j >= 8:
                            pe.wait_ge(kept, j - 7)
                        for k in range(KD):
                            t = nc.tensor.transpose(ps[j % 8][:, k * P:(k + 1) * P], y[:, j, k * 128:(k + 1) * 128], ident[0:P, 0:P])
                        t.then_inc(turned, 1)

            @block.scalar
            def _(act):
                for j in range(NJ):
                    act.wait_ge(mult, j + 1)
                    nc.scalar.activation(h[:, j, :], ps[j % 8][0:P, 0:D], ACT.Copy, scale=dinv[:, j:j + 1]).then_inc(hs, 1)
                act.wait_ge(scaled, 1)
                for j in range(NJ):
                    nc.scalar.activation(parts[:, j, 0, :], h[:, j, :], ACT.Copy, scale=scale[:, 0:1]).then_inc(highs, 1)
                if not last_layer:
                    for j in range(NJ):
                        act.wait_ge(taken, j + 1)
                        nc.scalar.activation(y[:, j, :], y[:, j, :], ACT.Gelu_apprx_tanh).then_inc(active, 1)
                    for j in range(NJ):
                        act.wait_ge(turned, j + 1)
                        nc.scalar.activation(xnT[:, :, j, :], ps[j % 8][:, 0:KD * P].rearrange("q (k p) -> q k p", k=KD),
                                             ACT.Copy).then_inc(kept, 1)

            @block.vector
            def _(dve):
                link = chain(dve, own)
                for j in range(NJ):
                    dve.wait_ge(hs, j + 1)
                    last = nc.vector.tensor_reduce(big[:, j:j + 1], h[:, j, :], AX.X, ALU.max, apply_absolute_value=True)
                link(last)
                nc.vector.tensor_reduce(big1[:, :], big[:, :], AX.X, ALU.max).then_inc(big_ready, 1)
                dve.wait_ge(big_turned, 1)
                link(nc.vector.tensor_reduce(bigT[:, 0:1], ps[0][0:1, 0:P], AX.X, ALU.max))
                link(nc.vector.tensor_scalar(bigT[:, 0:1], bigT[:, 0:1], 1e-30, None, ALU.max))
                link(nc.vector.reciprocal(bigT[:, 1:2], bigT[:, 0:1]))
                nc.vector.tensor_scalar(bigT[:, 1:2], bigT[:, 1:2], TOP, None, ALU.mult).then_inc(top_ready, 1)
                dve.wait_ge(top_spread, 1)
                nc.vector.tensor_scalar(back[:, :], ps[1][0:P, 0:1], 1.0 / TOP, None, ALU.mult)
                link(nc.vector.tensor_copy(scale[:, :], ps[1][0:P, 1:2]))
                nc.vector.tensor_scalar(out_scale[:, :], dinv[:, :], back[:, 0:1], None, ALU.mult).then_inc(scaled, 1)
                for j in range(NJ):
                    dve.wait_ge(highs, j + 1)
                    nc.vector.scalar_tensor_tensor(out=parts[:, j, 1, :], in0=h[:, j, :], scalar=scale[:, 0:1],
                                                   in1=parts[:, j, 0, :], op0=ALU.mult, op1=ALU.subtract).then_inc(split, 1)
                dve.wait_ge(w_in, 32)
                for n, (lo, hi) in enumerate(PASSES):
                    dve.wait_ge(used, (n + 1) * NJ)
                    for j in range(lo, hi):
                        i = j - lo
                        nc.vector.scalar_tensor_tensor(out=y[:, j, :], in0=ps[i // 2][0:P, i % 2 * D:(i % 2 + 1) * D],
                                                       scalar=out_scale[:, j:j + 1], in1=bias[:, :], op0=ALU.mult, op1=ALU.add).then_inc(taken, 1)
                        if last_layer:
                            dve.wait_ge(taken, j + 1)
                            nc.vector.tensor_tensor(x[:, j, :], x[:, j, :], y[:, j, :], ALU.add).then_inc(active, 1)
                if last_layer:
                    dve.wait_ge(active, NJ)

    CAP = max(1, -(-5 * N // (4 * NEXP)))
    TT = 4
    RL = -(-CAP // TT)
    ROOM = TT * RL
    X1F = 1024
    FT = X1F // 128
    FMAX = 3.4028234663852886e38

    def layer1_ffn():
        buf, ybuf = dram("buf", (NEXP * ROOM, D)), dram("ybuf", (NEXP * ROOM, D))
        with ExitStack() as outer:
            sbo = sb_in(outer, "f1_")
            share = sbo("share", [P, NJ])
            slot_out = sbo("slot_out", [P, NJ], I32)
            with ExitStack() as ctx:
                sb, sem = sb_in(ctx, "g1_"), sem_in(ctx, "g1_")
                xn = sb("xn", [P, NJ, D])
                norm_transpose("n3_", xn)
                wg, bg = sb("wg", [128, KD, NEXP]), sb("bg", [P, NEXP])
                lg = sb("lg", [P, NJ, NEXP])
                top8, idx8 = sb("top8", [P, NJ, 8]), sb("idx8", [P, NJ, 8], U32)
                idxf, red, hit = sb("idxf", [P, NJ]), sb("red", [P, NJ]), sb("hit", [P, NJ, NEXP])
                cum = sb("cum", [P, NJ, NEXP])
                posf, kept, slotf = sb("posf", [P, NJ]), sb("kept", [P, NJ]), sb("slotf", [P, NJ])
                slot_in = sb("slot_in", [P, NJ], I32)
                iota_i, iota = sb("iota_i", [P, NEXP], I32), sb("iota", [P, NEXP])
                zero = sb("zero", [RL, NEXP * TT * D])
                g_in, made, gated, own, zeroed = sem("g_in"), sem("made"), sem("gated"), sem("own"), sem("zeroed")
                less, exps, lane_tot, lane_base = sem("less"), sem("exps"), sem("lane_tot"), sem("lane_base")
                slots_ready, sent, zset = sem("slots_ready"), sem("sent"), sem("zset")
                block = ctx.enter_context(nc.Block())

                @block.sync
                def _(sp):
                    sp.dma_start(wg[:, :, :], a["L1_ffn_gate_w"].rearrange("(k q) e -> q k e", k=KD)).then_inc(g_in, 16)
                    sp.dma_start(bg[:, :], a["L1_ffn_gate_b"].unsqueeze(0).to_broadcast([P, NEXP])).then_inc(g_in, 16)
                    sp.wait_ge(zset, 1)
                    sp.dma_start(buf.rearrange("(p r) d -> p (r d)", p=RL), zero[:, :]).then_inc(zeroed, 16)

                @block.gpsimd
                def _(pool):
                    pool.memset(zero[:, :], 0.0).then_inc(zset, 1)
                    pool.iota(iota_i[:, :], [[1, NEXP]], base=0, channel_multiplier=0).then_inc(made, 1)
                    pool.wait_ge(zeroed, 16)
                    pool.wait_ge(slots_ready, 1)
                    for j in range(NJ):
                        pool.indirect_dma_start(buf, bass.IndirectOffsetOnAxis(ap=slot_in[:, j:j + 1].bitcast(U32), axis=0),
                                                xn[:, j, :], None, bounds_check=NEXP * ROOM - 1, oob_is_err=False).then_inc(sent, 16)
                    pool.wait_ge(sent, 16 * NJ)

                @block.tensor
                def _(pe):
                    pe.wait_ge(g_in, 32)
                    for j in range(NJ):
                        for k in range(KD):
                            m = nc.tensor.matmul(ps[0][0:P, j * NEXP:(j + 1) * NEXP], xnT[:, k, j, :], wg[:, k, :],
                                                 start=k == 0, stop=k == KD - 1)
                    m.then_inc(gated, 1)
                    pe.wait_ge(lane_tot, 1)
                    nc.tensor.matmul(ps[1][0:P, 0:NEXP], before[:, :], cum[:, NJ - 1, :], start=True, stop=True).then_inc(lane_base, 1)

                @block.scalar
                def _(act):
                    act.wait_ge(less, 1)
                    nc.scalar.activation(lg[:, :, :], lg[:, :, :], ACT.Exp).then_inc(exps, 1)

                @block.vector
                def _(dve):
                    link = chain(dve, own)
                    wide = lambda t: t.unsqueeze(1).to_broadcast([P, NJ, NEXP])
                    each = lambda t: t.unsqueeze(2).to_broadcast([P, NJ, NEXP])
                    dve.wait_ge(g_in, 32)
                    dve.wait_ge(gated, 1)
                    link(nc.vector.tensor_tensor(lg[:, :, :], ps[0][0:P, 0:NJ * NEXP].rearrange("p (j e) -> p j e", e=NEXP), wide(bg[:, :]), ALU.add))
                    link(nc.vector.tensor_reduce(red[:, :], lg[:, :, :], AX.X, ALU.max))
                    nc.vector.tensor_tensor(lg[:, :, :], lg[:, :, :], each(red[:, :]), ALU.subtract).then_inc(less, 1)
                    dve.wait_ge(exps, 1)
                    link(nc.vector.tensor_reduce(red[:, :], lg[:, :, :], AX.X, ALU.add))
                    link(nc.vector.reciprocal(red[:, :], red[:, :]))
                    link(nc.vector.tensor_tensor(lg[:, :, :], lg[:, :, :], each(red[:, :]), ALU.mult))
                    for j in range(NJ):
                        last = nc.vector.max(top8[:, j, :], lg[:, j, :])
                    link(last)
                    for j in range(NJ):
                        last = nc.vector.max_index(idx8[:, j, :], top8[:, j, :], lg[:, j, :])
                    link(last)
                    dve.wait_ge(made, 1)
                    nc.vector.tensor_copy(iota[:, :], iota_i[:, :])
                    link(nc.vector.tensor_copy(idxf[:, :], idx8[:, :, 0]))
                    link(nc.vector.tensor_tensor(hit[:, :, :], wide(iota[:, :]), each(idxf[:, :]), ALU.is_equal))
                    for e in range(NEXP):
                        last = nc.vector.tensor_tensor_scan(cum[:, :, e], ones[:, 0:NJ], hit[:, :, e], 0.0, ALU.mult, ALU.add)
                    last.then_inc(lane_tot, 1)
                    dve.wait_ge(lane_base, 1)
                    link(nc.vector.tensor_tensor(lg[:, :, :], cum[:, :, :], wide(ps[1][0:P, 0:NEXP]), ALU.add))
                    link(nc.vector.tensor_tensor(lg[:, :, :], lg[:, :, :], hit[:, :, :], ALU.mult))
                    link(nc.vector.tensor_reduce(posf[:, :], lg[:, :, :], AX.X, ALU.add))
                    link(nc.vector.tensor_scalar(posf[:, :], posf[:, :], 1.0, None, ALU.subtract))
                    link(nc.vector.tensor_scalar(kept[:, :], posf[:, :], float(CAP), None, ALU.is_lt))
                    link(nc.vector.tensor_tensor(share[:, :], top8[:, :, 0], kept[:, :], ALU.mult))
                    link(nc.vector.tensor_scalar(posf[:, :], posf[:, :], float(CAP - 1), None, ALU.min))
                    link(nc.vector.scalar_tensor_tensor(out=slotf[:, :], in0=idxf[:, :], scalar=float(ROOM), in1=posf[:, :],
                                                        op0=ALU.mult, op1=ALU.add))
                    nc.vector.tensor_copy(slot_out[:, :], slotf[:, :])
                    link(nc.vector.tensor_scalar(kept[:, :], kept[:, :], -SKIP, SKIP, ALU.mult, ALU.add))
                    link(nc.vector.tensor_tensor(slotf[:, :], slotf[:, :], kept[:, :], ALU.add))
                    nc.vector.tensor_copy(slot_in[:, :], slotf[:, :]).then_inc(slots_ready, 1)
            with ExitStack() as ctx:
                sb, sem = sb_in(ctx, "e1_"), sem_in(ctx, "e1_")
                w1, w2 = sb("w1", [128, 2, KD, X1F]), sb("w2", [128, 2, FT, D])
                b1, b2 = sb("b1", [128, 2, FT]), sb("b2", [1, 2, D])
                tok = sb("tok", [RL, 2, TT, D])
                tokT = sb("tokT", [128, 2, KD, ROOM])
                hT = sb("hT", [128, 2, FT, ROOM])
                y = sb("y", [RL, 2, TT, D])
                in_ = [sem("in0"), sem("in1")]
                out_ = [sem("out0"), sem("out1")]
                turned, tok_kept, up, relued, down, y_kept = (sem(n) for n in ("turned", "tok_kept", "up", "relued", "down", "y_kept"))
                block = ctx.enter_context(nc.Block())
                LOADS = 5 * 16

                @block.sync
                def _(sp):
                    for e in range(NEXP):
                        u, rows = e % 2, slice(e * ROOM, (e + 1) * ROOM)
                        if e >= 2:
                            sp.wait_ge(down, TT * (e - 1))
                        sp.dma_start(tok[:, u, :, :], buf[rows, :].rearrange("(i t) d -> i t d", t=TT)).then_inc(in_[u], 16)
                        sp.dma_start(w1[:, u, :, :], a["L1_ffn_w1"][e].rearrange("(k q) f -> q k f", k=KD)).then_inc(in_[u], 16)
                        sp.dma_start(b1[:, u, :], a["b1_1_cols"][:, e, :]).then_inc(in_[u], 16)
                        sp.dma_start(w2[:, u, :, :], a["L1_ffn_w2"][e].rearrange("(m q) d -> q m d", m=FT)).then_inc(in_[u], 16)
                        sp.dma_start(b2[:, u, :], a["L1_ffn_b2"][e:e + 1, :]).then_inc(in_[u], 16)

                @block.gpsimd
                def _(pool):
                    for e in range(NEXP):
                        u = e % 2
                        pool.wait_ge(y_kept, TT * (e + 1))
                        pool.dma_start(ybuf[e * ROOM:(e + 1) * ROOM, :].rearrange("(i t) d -> i t d", t=TT), y[:, u, :, :]).then_inc(out_[u], 16)
                    for u in range(2):
                        pool.wait_ge(out_[u], 16 * NEXP // 2)

                @block.tensor
                def _(pe):
                    for e in range(NEXP):
                        u = e % 2
                        pe.wait_ge(in_[u], LOADS * (e // 2 + 1))
                        for t in range(TT):
                            i = e * TT + t
                            if i >= 2:
                                pe.wait_ge(tok_kept, i - 1)
                            for k in range(KD):
                                m = nc.tensor.transpose(ps[i % 2][:, k * 128:k * 128 + RL], tok[:, u, t, k * 128:(k + 1) * 128], ident[0:RL, 0:RL])
                            m.then_inc(turned, 1)
                        pe.wait_ge(tok_kept, TT * (e + 1))
                        for f in range(FT):
                            i = e * FT + f
                            if i >= 3:
                                pe.wait_ge(relued, i - 2)
                            for k in range(KD):
                                m = nc.tensor.matmul(ps[2 + i % 3][:, 0:ROOM], w1[:, u, k, f * 128:(f + 1) * 128], tokT[:, u, k, :],
                                                     start=k == 0, stop=k == KD - 1)
                            m.then_inc(up, 1)
                        pe.wait_ge(relued, FT * (e + 1))
                        for t in range(TT):
                            i = e * TT + t
                            if i >= 3:
                                pe.wait_ge(y_kept, i - 2)
                            for f in range(FT):
                                nc.tensor.matmul(ps[5 + i % 3][0:RL, 0:D], hT[:, u, f, t * RL:(t + 1) * RL], w2[:, u, f, :],
                                                 start=f == 0, stop=False)
                            nc.tensor.matmul(ps[5 + i % 3][0:RL, 0:D], ones[0:1, 0:RL], b2[:, u, :], start=False, stop=True).then_inc(down, 1)

                @block.scalar
                def _(act):
                    for e in range(NEXP):
                        u = e % 2
                        act.wait_ge(in_[u], LOADS * (e // 2 + 1))
                        for f in range(FT):
                            i = e * FT + f
                            act.wait_ge(up, i + 1)
                            nc.scalar.activation(hT[:, u, f, :], ps[2 + i % 3][:, 0:ROOM], ACT.Relu, bias=b1[:, u, f:f + 1]).then_inc(relued, 1)

                @block.vector
                def _(dve):
                    for e in range(NEXP):
                        u = e % 2
                        for t in range(TT):
                            i = e * TT + t
                            dve.wait_ge(turned, i + 1)
                            nc.vector.tensor_copy(tokT[:, u, :, t * RL:(t + 1) * RL], ps[i % 2][:, 0:KD * 128].rearrange(
                                "q (k i) -> q k i", k=KD)[:, :, 0:RL]).then_inc(tok_kept, 1)
                        if e >= 2:
                            dve.wait_ge(out_[u], 16 * (e // 2))
                        for t in range(TT):
                            i = e * TT + t
                            dve.wait_ge(down, i + 1)
                            nc.vector.tensor_copy(y[:, u, t, :], ps[5 + i % 3][0:RL, 0:D]).then_inc(y_kept, 1)
            with ExitStack() as ctx:
                sb, sem = sb_in(ctx, "r1_"), sem_in(ctx, "r1_")
                back = sb("back", [P, NJ, D])
                clean = sb("clean", [P, 2, D])
                mask = sb("mask", [P, 2, 3, D], I32)
                high, low = sb("high", [P, D]), sb("low", [P, D])
                landed = [sem(f"landed{i}") for i in range(5)]
                own, done, sent = sem("own"), sem("done"), sem("sent")
                block = ctx.enter_context(nc.Block())

                @block.gpsimd
                def _(pool):
                    for j in range(NJ):
                        pool.indirect_dma_start(back[:, j, :], None, ybuf,
                                                bass.IndirectOffsetOnAxis(ap=slot_out[:, j:j + 1].bitcast(U32), axis=0)).then_inc(landed[j // 5], 16)

                @block.vector
                def _(dve):
                    link = chain(dve, own)
                    nc.vector.memset(high[:, :], 1e4)
                    link(nc.vector.memset(low[:, :], -1e4))
                    for j in range(NJ):
                        u, row = j % 2, back[:, j, :]
                        dve.wait_ge(landed[j // 5], 80)
                        nc.vector.memset(clean[:, u, :], 0.0)
                        link(nc.vector.tensor_scalar(row, row, share[:, j:j + 1], None, ALU.mult))
                        nc.vector.tensor_tensor(mask[:, u, 0, :], row, row, ALU.is_equal)
                        nc.vector.tensor_scalar(mask[:, u, 1, :], row, FMAX, None, ALU.is_gt)
                        link(nc.vector.tensor_scalar(mask[:, u, 2, :], row, -FMAX, None, ALU.is_lt))
                        link(nc.vector.copy_predicated(clean[:, u, :], mask[:, u, 0, :], row))
                        link(nc.vector.copy_predicated(clean[:, u, :], mask[:, u, 1, :], high[:, :]))
                        link(nc.vector.copy_predicated(clean[:, u, :], mask[:, u, 2, :], low[:, :]))
                        nc.vector.tensor_tensor(x[:, j, :], x[:, j, :], clean[:, u, :], ALU.add).then_inc(done, 1)

                @block.sync
                def _(sp):
                    out_rows = out.rearrange("(p j) d -> p j d", j=NJ)
                    for q in range(5):
                        sp.wait_ge(done, 5 * (q + 1))
                        sp.dma_start(out_rows[:, 5 * q:5 * q + 5, :], x[:, 5 * q:5 * q + 5, :]).then_inc(sent, 16)
                    sp.wait_ge(sent, 5 * 16)

    def with_norm(tag):
        with ExitStack() as ctx:
            norm_transpose(tag, sb_in(ctx, tag)("xn", [P, NJ, D]))

    with top:
        constants()
        with_norm("n0_")
        layer0_gnn()
        recycle()
        with_norm('n1_')
        layer0_ffn()
        recycle()
        with_norm('n2_')
        build_adjacency()
        recycle()
        convolve("c1_", "L1_gnn_W1", "L1_gnn_b1", False)
        convolve("c2_", "L1_gnn_W2", "L1_gnn_b2", False)
        convolve("c3_", "L1_gnn_W3", "L1_gnn_b3", True)
        recycle()
        layer1_ffn()


def kernel(**inputs):
    import numpy as np
    import concourse.bacc as bacc
    from concourse.bass_utils import run_bass_kernel_spmd

    arrays = {k: np.ascontiguousarray(v) for k, v in inputs.items() if k != "edge_attr_16"}
    arrays["src_cols"] = np.ascontiguousarray(np.asarray(inputs["src"]).reshape(P, NB, G).transpose(1, 2, 0).reshape(NB, G * P))
    attr = np.asarray(inputs["edge_attr_16"]).reshape(P, EC // 8, 8, FE)
    arrays["edge_attr_cols"] = np.ascontiguousarray(attr.transpose(2, 3, 1, 0).reshape(8 * FE, EC // 8, P))
    arrays["b1_0_cols"] = np.ascontiguousarray(np.asarray(inputs["L0_ffn_b1"]).reshape(NEXP * X0F // 128, 128).T)
    arrays["b1_1_cols"] = np.ascontiguousarray(np.asarray(inputs["L1_ffn_b1"]).reshape(NEXP, 8, 128).transpose(2, 0, 1))
    nc = bacc.Bacc("TRN2", target_bir_lowering=False, num_devices=1)
    aps = {k: nc.dram_tensor("in_" + k, v.shape, mybir.dt.from_np(v.dtype), kind="ExternalInput").ap() for k, v in arrays.items()}
    out = nc.dram_tensor("out", (N, D), F32, kind="ExternalOutput").ap()
    build(nc, aps, out)
    r = run_bass_kernel_spmd(nc, [{"in_" + k: v for k, v in arrays.items()}], core_ids=[0])
    return r.results[0]["out"]
```
